# Optimizing a Trainium2 kernel written in Bass

```python
import numpy as np
import jax
import jax.numpy as jnp

def _softmax(x, axis=-1):
    return jax.nn.softmax(x, axis=axis)
def _gelu(x):
    return jax.nn.gelu(x, approximate=True)
def _silu(x):
    return jax.nn.silu(x)
def _sigmoid(x):
    return jax.nn.sigmoid(x)
def _layernorm(x, axis=-1, eps=1e-5):
    m = jnp.mean(x, axis=axis, keepdims=True)
    v = jnp.var(x, axis=axis, keepdims=True)
    return (x - m) / jnp.sqrt(v + eps)
def _scatter_add(tgt, idx, src, axis=0):
    return tgt.at[idx].add(src)
def _segment_sum(src, seg, n):
    return jax.ops.segment_sum(src, seg, n)

kernel_name = 'mk_adj_preln_d2_adj_512_12f1bc'

def setup_inputs(seed: int = 0):
    np.random.seed(seed)
    _w = jnp.asarray
    def _rec_inputs():
        import jax
        import jax.numpy as jnp
        _gk = jax.random.key(seed)
        x = -0.0002928 + 1 * jax.random.normal(jax.random.fold_in(_gk, 1), (64, 256, 512), jnp.float32)
        _w = (1.0 + jnp.arange(256, dtype=jnp.float32)) ** -0.5
        _w = _w / _w.mean()
        _pij = jnp.clip(0.015625 * _w[:, None] * _w[None, :], 0.0, 1.0)
        _a = jax.random.uniform(jax.random.fold_in(_gk, 2), (256, 256)) < _pij
        _a = jnp.logical_or(_a, jnp.eye(256, dtype=bool))
        _af = _a.astype(jnp.float32)
        adj = _af
        return x, adj
    x, adj = _rec_inputs()
    def _L0_gnn_setup():
        import jax, jax.numpy as jnp
        import numpy as np
        B, N, D = (4, 2048, 512)
        H, HD = (8, 64)
        key = jax.random.key(seed)
        ks = jax.random.split(key, 6)
        x = jax.random.normal(ks[0], (B, N, D), dtype=jnp.float32)
        adj = (jax.random.uniform(ks[1], (N, N)) < 0.1).astype(jnp.float32)
        adj = jnp.maximum(adj, jnp.eye(N, dtype=jnp.float32))
        s = 0.02
        Wq = jax.random.normal(ks[2], (D, H * HD), dtype=jnp.float32) * s
        Wk = jax.random.normal(ks[3], (D, H * HD), dtype=jnp.float32) * s
        Wv = jax.random.normal(ks[4], (D, H * HD), dtype=jnp.float32) * s
        bq = jnp.zeros((H * HD,), dtype=jnp.float32)
        bk = jnp.zeros((H * HD,), dtype=jnp.float32)
        bv = jnp.zeros((H * HD,), dtype=jnp.float32)
        return {'x': x, 'adj': adj, 'Wq': Wq, 'bq': bq, 'Wk': Wk, 'bk': bk, 'Wv': Wv, 'bv': bv}
    _L0_gnn_all = _L0_gnn_setup()
    _L0_gnn_in = {k: v for k, v in _L0_gnn_all.items() if k in ('Wq', 'bq', 'Wk', 'bk', 'Wv', 'bv', )}
    del _L0_gnn_all

    def _L1_gnn_setup():
        import jax, jax.numpy as jnp
        import numpy as np
        B, N, D = (8, 2048, 512)
        key = jax.random.key(seed)
        k1, k2, k3, k4, k5 = jax.random.split(key, 5)
        neuron_states = jax.random.normal(k1, (B, N, D), dtype=jnp.float32)
        adjacency = jax.random.randint(k2, (N, N), 0, 2).astype(jnp.float32)
        scale = 1.0 / np.sqrt(D)
        Wq = jax.random.normal(k3, (D, D), dtype=jnp.float32) * scale
        Wk = jax.random.normal(k4, (D, D), dtype=jnp.float32) * scale
        Wv = jax.random.normal(k5, (D, D), dtype=jnp.float32) * scale
        return {'neuron_states': neuron_states, 'adjacency': adjacency, 'Wq': Wq, 'Wk': Wk, 'Wv': Wv}
    _L1_gnn_all = _L1_gnn_setup()
    _L1_gnn_in = {k: v for k, v in _L1_gnn_all.items() if k in ('Wq', 'Wk', 'Wv', )}
    del _L1_gnn_all

    return {
        "x": x,
        "adj": adj,
        "L0_gnn_Wq": _L0_gnn_in["Wq"],
        "L0_gnn_bq": _L0_gnn_in["bq"],
        "L0_gnn_Wk": _L0_gnn_in["Wk"],
        "L0_gnn_bk": _L0_gnn_in["bk"],
        "L0_gnn_Wv": _L0_gnn_in["Wv"],
        "L0_gnn_bv": _L0_gnn_in["bv"],
        "L1_gnn_Wq": _L1_gnn_in["Wq"],
        "L1_gnn_Wk": _L1_gnn_in["Wk"],
        "L1_gnn_Wv": _L1_gnn_in["Wv"],
    }

def reference(x, adj, L0_gnn_Wq, L0_gnn_bq, L0_gnn_Wk, L0_gnn_bk, L0_gnn_Wv, L0_gnn_bv, L1_gnn_Wq, L1_gnn_Wk, L1_gnn_Wv):
    import jax
    import jax.numpy as jnp
    def _L0_gnn_ref(x, adj, Wq, bq, Wk, bk, Wv, bv):
        import jax, jax.numpy as jnp
        import numpy as np
        B, N, D = (4, 2048, 512)
        H, HD = (8, 64)
        b, n, _ = x.shape
        q = (x @ Wq + bq).reshape(b, n, H, HD)
        k = (x @ Wk + bk).reshape(b, n, H, HD)
        v = (x @ Wv + bv).reshape(b, n, H, HD)
        scores = jnp.einsum('bihd,bjhd->bhij', q, k) / jnp.sqrt(jnp.float32(HD))
        mask = jnp.where(adj == 0, jnp.float32(-1000000000.0), jnp.float32(0.0))
        scores = scores + mask[None, None, :, :]
        weights = jax.nn.softmax(scores, axis=-1)
        out = jnp.einsum('bhij,bjhd->bihd', weights, v)
        return out.reshape(b, n, H * HD)

    def _L1_gnn_ref(neuron_states, adjacency, Wq, Wk, Wv):
        import jax, jax.numpy as jnp
        import numpy as np
        B, N, D = (8, 2048, 512)
        q = jnp.einsum('bnd,ed->bne', neuron_states, Wq)
        k = jnp.einsum('bnd,ed->bne', neuron_states, Wk)
        v = jnp.einsum('bnd,ed->bne', neuron_states, Wv)
        rel = jnp.einsum('bnd,bmd->bnm', q, k)
        rel = adjacency.T[None, :, :] * rel
        rel = rel / jnp.linalg.norm(rel, axis=2, keepdims=True)
        return jnp.einsum('bnm,bmd->bnd', rel, v)

    h = jnp.maximum(_layernorm(x, axis=-1), 0.0)
    x = x + _L0_gnn_ref(h, adj, L0_gnn_Wq, L0_gnn_bq, L0_gnn_Wk, L0_gnn_bk, L0_gnn_Wv, L0_gnn_bv)
    h = jnp.maximum(_layernorm(x, axis=-1), 0.0)
    x = x + _L1_gnn_ref(h, adj, L1_gnn_Wq, L1_gnn_Wk, L1_gnn_Wv)
    return x


_drawn_inputs = setup_inputs


def setup_inputs(seed=0):
    import zlib

    import numpy as np

    out = dict(_drawn_inputs(seed))
    spreads = {'L0_gnn_bq': (0.0, 0.8), 'L0_gnn_bk': (0.0, 0.8), 'L0_gnn_bv': (0.0, 0.1)}
    factors = {'L0_gnn_Wq': 3.16, 'L0_gnn_Wk': 2.961}
    for name, (base, spread) in spreads.items():
        noise = np.random.default_rng([zlib.crc32(name.encode()), seed]).standard_normal(out[name].shape)
        drawn = base * np.exp(spread * noise) if base else spread * noise
        out[name] = jnp.asarray(drawn.astype(out[name].dtype))
    for name, factor in factors.items():
        out[name] = (out[name] * factor).astype(out[name].dtype)
    return out
```

```python
import concourse.bass as bass
from concourse import mybir
from contextlib import ExitStack


def adjacency_attention_two_layers(
    nc: bass.Bass,
    x: bass.AP,
    adj: bass.AP,
    wq0: bass.AP,
    bq0: bass.AP,
    wk0: bass.AP,
    bk0: bass.AP,
    wv0: bass.AP,
    bv0: bass.AP,
    wq1: bass.AP,
    wk1: bass.AP,
    wv1: bass.AP,
    out: bass.AP,
):
    fp32 = mybir.dt.float32
    fp16 = mybir.dt.float16
    ALU = mybir.AluOpType
    ACT = mybir.ActivationFunctionType

    GRAPHS, N, D = x.shape
    HEADS, HD = 8, 64
    P = 128
    PAIRS = GRAPHS // 2
    TOK = 2 * N
    TILES = TOK // P
    NT = N // P
    KT = D // P
    UNITS = 2 * HEADS
    EPS = 1e-5
    WS = 32.0
    QS = -WS * HD ** -0.5
    SCORE = -1.0 / (QS * WS * HD ** 0.5)
    MASK = 1.0e9 / SCORE
    SPLIT = ((0, 0), (0, 1), (1, 0))
    BIG = 3.0e38

    SLOTS = [("v", 0), ("v", 1), ("v", 2), ("v", 3), ("rq", 0), ("q", 0), ("rq", 1), ("k", 0),
             ("rq", 2), ("q", 1), ("rq", 3), ("k", 1), ("rv", 0), ("rel", 0), ("q", 2), ("rel", 1),
             ("k", 2), ("rv", 1), ("rv", 2), ("q", 3), ("rv", 3), ("k", 3),
             ("out", 0), ("out", 1), ("out", 2), ("out", 3)]
    SCORES_AT = [0, 1, 2, 3, 5, 6, 7, 8, 10, 11, 12, 13, 15, 16, 17, 18]
    EXTRA = {0: [("ht", c) for c in range(KT)], 4: [("rht", c) for c in range(KT)],
             14: [("rel_scale", 0)], 16: [("rel_scale", 1)],
             18: [("relt", 0)], 20: [("relt", 1)],
             9: [("ln0_stats", 0)], 11: [("ln0_scale", 0)], 12: [("ln0_apply", 0)],
             23: [("ln1_stats", 0)], 24: [("ln1_scale", 0)], 25: [("ln1_apply", 0)]}
    PLAN = [("turn", 0)]
    for at, big in enumerate(SLOTS):
        PLAN += EXTRA.get(at, [])
        if at in SCORES_AT:
            PLAN.append(("scores", SCORES_AT.index(at)))
        if at - 2 in SCORES_AT:
            PLAN.append(("probs_t", SCORES_AT.index(at - 2)))
        if at in SCORES_AT:
            PLAN.append(("exp", SCORES_AT.index(at)))
        PLAN.append(big)
        if at - 3 in SCORES_AT:
            u = SCORES_AT.index(at - 3)
            PLAN.append(("pv", u))
            if u % 4 == 3:
                PLAN.append(("norm", u // 4))
    PROJECT = [st for st in PLAN if st[0] in ("ht", "q", "k", "v")]
    RELATE = [st for st in PLAN if st[0] in ("rht", "rq", "rv", "rel", "relt", "out")]
    HALVED = [st for st in RELATE if st[0] in ("rht", "rq", "rv", "relt")]
    NPC, NRC, NRH = len(PROJECT), len(RELATE), len(HALVED)

    def unit(u):
        return u // 4, (u % 4) // 2, u % 2

    xv = x.rearrange("(n g) (t p) d -> n p (g t) d", g=2, p=P)
    ov = out.rearrange("(n g) (t p) d -> n p (g t) d", g=2, p=P)

    ctx = ExitStack()
    with ctx:
        def sb(name, shape, dt=fp32):
            return ctx.enter_context(nc.sbuf_tensor(name, shape, dt))

        def bank(name, shape):
            return ctx.enter_context(nc.psum_tensor(name, shape, fp32))

        def sem(name):
            return ctx.enter_context(nc.semaphore(name))

        wq = sb("wq", [P, 2, KT, D], fp16)
        wk = sb("wk", [P, 2, KT, D], fp16)
        wv = sb("wv", [P, 2, KT, D], fp16)
        wm = sb("wm", [P, 2, KT, D], fp16)
        wvt = sb("wvt", [P, 2, KT, D], fp16)
        bq = sb("bq", [P, KT])
        bk = sb("bk", [P, KT])
        bv = sb("bv", [P, D])
        ident = sb("ident", [P, P])
        adj_in = sb("adj_in", [P, NT, N])
        mask = sb("mask", [P, NT, N])
        adj_t = sb("adj_t", [P, NT, N])
        half = sb("half", [P, TILES])
        x_in = sb("x_in", [P, TILES, D])
        h0 = sb("h0", [P, TILES, D])
        h0t = sb("h0t", [P, 2, KT, TOK], fp16)
        q_st = sb("q_st", [P, KT, 2, TOK], fp16)
        k_st = sb("k_st", [P, KT, 2, 2, TOK], fp16)
        v_sum = sb("v_sum", [P, 2, D])
        v = sb("v", [P, 2, 2, TILES, D], fp16)
        x_res = sb("x_res", [P, 2, TILES, D])
        masked = sb("masked", [P, 2, NT, N])
        neg_max = sb("neg_max", [P, 2, NT])
        probs = sb("probs", [P, 2, NT, N])
        row_sum = sb("row_sum", [P, 2, TILES, 2])
        row_inv = sb("row_inv", [P, 2, TILES, 2])
        probs_t = sb("probs_t", [P, 2, 2, NT, N], fp16)
        attn = sb("attn", [P, 2, TILES * 2, HD])
        h1 = sb("h1", [P, TILES, D])
        h1t = sb("h1t", [P, 2, KT, TOK], fp16)
        rq = sb("rq", [P, 2, KT, TOK], fp16)
        rv = sb("rv", [P, 2, TILES, D], fp16)
        rel = sb("rel", [P, 2, NT, N])
        rel_n = sb("rel_n", [P, 2, NT, N])
        rel_t = sb("rel_t", [P, 2, 2, NT, N], fp16)
        squares = sb("squares", [P, 2, NT, N])
        sq_sum = sb("sq_sum", [P, 2, NT])
        sq_pow = sb("sq_pow", [P, 2, NT])
        sq_work = sb("sq_work", [P, NT])
        rel_inv = sb("rel_inv", [P, 2, NT])
        result = sb("result", [P, 2, D])
        stats = sb("stats", [P, 2, TILES, 6])
        moments = sb("moments", [P, 2, TILES, 2])
        var = sb("var", [P, 2, TILES])
        guess = sb("guess", [P, 2, TILES])
        ln_work = sb("ln_work", [P, 2, TILES])
        rstd = sb("rstd", [P, 2, TILES])
        shift = sb("shift", [P, 2, TILES])

        S = [bank(f"S{i}", [P, NT, N]) for i in range(2)]
        PT = bank("PT", [P, NT, N])
        O = bank("O", [P, TILES * 2, HD])
        PB = [bank(f"PB{i}", [P, TOK]) for i in range(2)]
        RB = [bank(f"RB{i}", [P, TOK]) for i in range(2)]

        x_loaded = sem("x_loaded")
        res_loaded = [sem(f"res_loaded{i}") for i in range(2)]
        w_loaded = [sem(f"w_loaded{i}") for i in range(6)]
        small_loaded = sem("small_loaded")
        adj_loaded = sem("adj_loaded")
        k_doubled = [sem(f"k_doubled{m}") for m in range(KT)]
        stored = [sem(f"stored{i}") for i in range(2)]
        consts_ready = sem("consts_ready")
        ident_zero = sem("ident_zero")
        w_high = sem("w_high")
        w_low = sem("w_low")
        scaled = sem("scaled")
        setup_product = sem("setup_product")
        setup_high = sem("setup_high")
        setup_done = sem("setup_done")
        p_product = sem("p_product")
        p_high = sem("p_high")
        p_done = sem("p_done")
        v_low = sem("v_low")
        scored = sem("scored")
        maxed = sem("maxed")
        exped = sem("exped")
        transposed = sem("transposed")
        pt_high = sem("pt_high")
        pt_low = sem("pt_low")
        summed = sem("summed")
        inverted = sem("inverted")
        normed = sem("normed")
        residual = sem("residual")
        settled = sem("settled")
        r_product = sem("r_product")
        r_high = sem("r_high")
        r_done = sem("r_done")
        squared = sem("squared")
        rel_guess = sem("rel_guess")
        rel_steps = sem("rel_steps")
        rel_scale = sem("rel_scale")
        rel_normed = sem("rel_normed")
        ln_steps = [sem(f"ln_steps{i}") for i in range(2)]
        ln_var = [sem(f"ln_var{i}") for i in range(2)]
        ln_guess = [sem(f"ln_guess{i}") for i in range(2)]
        ln_scale = [sem(f"ln_scale{i}") for i in range(2)]
        ln_done = [sem(f"ln_done{i}") for i in range(2)]

        block = ctx.enter_context(nc.Block())

        def need(eng, semaphore, value):
            if not (isinstance(value, int) and value <= 0):
                eng.wait_ge(semaphore, value)

        def stages(s, last):
            if not isinstance(s, int):
                return True, True, True, True, True
            return s < last, 1 <= s <= last, s >= 2, s + 1 < last, s + 2 < last

        def turns(eng, turn, between):
            turn(0, 0)
            between()
            for s in range(1, 4):
                turn(s, s % 2)
            with eng.Fori(0, (PAIRS - 6) // 2) as i:
                for odd in range(2):
                    turn(2 * i + 4 + odd, odd)
            for s in range(PAIRS - 2, PAIRS + 2):
                turn(s, s % 2)

        @block.sync
        def _(sp):
            sp.dma_start(x_in[:, :, :], xv[0]).then_inc(x_loaded, 16)
            stage = [x_res[:, 0, :, :], x_res[:, 1, :, :], h1[:, :, :]]
            for n, w in enumerate((wq0, wk0, wv0)):
                sp.dma_start(stage[n], w.rearrange("(t p) n -> p t n", p=P)).then_inc(w_loaded[n], 16)
            sp.dma_start(adj_in[:, :, :], adj.rearrange("(t p) n -> p t n", p=P)).then_inc(adj_loaded, 16)
            for n, w in enumerate((wq1, wk1, wv1)):
                sp.wait_ge(w_low, n + 1)
                sp.dma_start(stage[n], w.rearrange("(t p) n -> p t n", p=P)).then_inc(w_loaded[3 + n], 16)
            sp.wait_ge(ln_done[0], 1)
            sp.dma_start(x_in[:, :, :], xv[1]).then_inc(x_loaded, 16)

            def between():
                sp.wait_ge(setup_done, 2 * KT + 1)

            def turn(s, odd):
                project, attend, relate, ln0, load = stages(s, PAIRS)
                a, l = s - 1, s - 2
                par = 1 - odd
                for kind, n in PLAN:
                    if kind == "turn" and attend:
                        if relate:
                            need(sp, r_done, NRC * l)
                        sp.dma_start(x_res[:, par, :, :], xv[a]).then_inc(res_loaded[par], 16)
                    elif kind == "k" and project:
                        sp.wait_ge(p_done, NPC * s + PROJECT.index(("k", n)) + 1)
                        for e in range(2):
                            own, other = slice(e * HD, (e + 1) * HD), slice((1 - e) * HD, (2 - e) * HD)
                            sp.dma_start(k_st[other, n, e, :, :], k_st[own, n, e, :, :]).then_inc(k_doubled[n], 16)
                    elif kind == "ln0_apply" and load:
                        sp.wait_ge(ln_done[0], s + 2)
                        sp.dma_start(x_in[:, :, :], xv[s + 2]).then_inc(x_loaded, 16)
                    elif kind == "out" and relate:
                        sp.wait_ge(r_done, NRC * l + RELATE.index(("out", n)) + 1)
                        sp.dma_start(ov[l][:, n, :], result[:, n % 2, :]).then_inc(stored[n % 2], 16)

            turns(sp, turn, between)
            for i in range(2):
                sp.wait_ge(stored[i], 16 * PAIRS * TILES // 2)

        @block.gpsimd
        def _(pool):
            nc.gpsimd.memset(ident[:, :], 0.0).then_inc(ident_zero, 1)
            nc.gpsimd.memset(half[:, :], -0.5).then_inc(consts_ready, 1)
            pool.wait_ge(ident_zero, 1)
            nc.gpsimd.affine_select(out=ident[:, :], in_=ident[:, :], compare_op=ALU.not_equal, fill=1.0,
                                    base=0, pattern=[[-1, P]], channel_multiplier=1).then_inc(consts_ready, 1)
            pool.wait_ge(consts_ready, 2)

            def ln_power(layer, count):
                pool.wait_ge(ln_var[layer], count)
                nc.gpsimd.tensor_tensor(guess[:, layer, :], var[:, layer, :], half[:, :],
                                        ALU.pow).then_inc(ln_guess[layer], 1)

            ln_power(0, 1)

            def turn(s, odd):
                project, attend, relate, ln0, _ = stages(s, PAIRS)
                a, l = s - 1, s - 2
                par = 1 - odd
                for kind, n in PLAN:
                    if kind == "v" and project:
                        pool.wait_ge(p_high, NPC * s + PROJECT.index(("v", n)) + 1)
                        nc.gpsimd.tensor_tensor(v[:, odd, 1, n, :], v_sum[:, n % 2, :], v[:, odd, 0, n, :],
                                                ALU.subtract).then_inc(v_low, 1)
                    elif kind == "ln0_scale" and ln0:
                        ln_power(0, s + 2)
                    elif kind == "ln1_scale" and attend:
                        ln_power(1, a + 1)
                    elif kind == "norm" and attend:
                        if n == 0:
                            pool.wait_ge(res_loaded[par], 8 * (a - par) + 16)
                        pool.wait_ge(normed, KT * a + n + 1)
                        cols = x_res[:, par, :, n * P:(n + 1) * P]
                        nc.gpsimd.tensor_tensor(cols, cols,
                                                attn[:, n % 2, :, :].rearrange("p (t e) d -> p t (e d)", e=2),
                                                ALU.add).then_inc(residual, 1)
                    elif kind == "rel" and relate:
                        pool.wait_ge(squared, 2 * l + n + 1)
                        nc.gpsimd.tensor_tensor(sq_pow[:, n, :], sq_sum[:, n, :], half[:, 0:NT],
                                                ALU.pow).then_inc(rel_guess, 1)
                        pool.wait_ge(rel_scale, 2 * l + n + 1)
                        need(pool, r_product, NRC * l)
                        nc.gpsimd.tensor_tensor(rel_n[:, n, :, :], rel[:, n, :, :],
                                                rel_inv[:, n, :].unsqueeze(2).broadcast_to([P, NT, N]),
                                                ALU.mult).then_inc(rel_normed, 1)

            turns(pool, turn, lambda: None)

        @block.scalar
        def _(act):
            act.dma_start(bq[:, :], bq0.rearrange("(m p) -> p m", p=P),
                          allow_slow_non_contiguous=True).then_inc(small_loaded, 16)
            act.dma_start(bk[:, :], bk0.rearrange("(m p) -> p m", p=P),
                          allow_slow_non_contiguous=True).then_inc(small_loaded, 16)
            act.dma_start(bv[:, :], bv0.partition_broadcast(P)).then_inc(small_loaded, 16)

            stage = [x_res[:, 0, :, :], x_res[:, 1, :, :], h1[:, :, :]]
            for n, (w, scale) in enumerate(((wq, QS), (wk, WS), (wv, WS))):
                act.wait_ge(w_loaded[n], 16)
                nc.scalar.activation(w[:, 0, :, :], stage[n], ACT.Copy, scale=scale).then_inc(w_high, 1)

            def ln_apply(layer, src, dst, count):
                act.wait_ge(ln_scale[layer], count)
                for t in range(TILES):
                    ins = nc.scalar.activation(dst[:, t, :], src[:, t, :], ACT.Identity,
                                               scale=rstd[:, layer, t:t + 1], bias=shift[:, layer, t:t + 1])
                ins.then_inc(ln_done[layer], 1)

            ln_apply(0, x_in[:, :, :], h0, 1)
            act.wait_ge(scaled, 1)

            def between():
                for n in range(2 * KT):
                    act.wait_ge(setup_product, n + 1)
                    dst = (wm if n < KT else wvt)[:, 0, n % KT, :]
                    nc.scalar.activation(dst, S[n % 2][:, :, :], ACT.Copy, scale=WS).then_inc(setup_high, 1)

            def turn(s, odd):
                project, attend, relate, ln0, _ = stages(s, PAIRS)
                a, l = s - 1, s - 2
                par = 1 - odd
                for kind, n in PLAN:
                    if kind in ("ht", "q", "k") and project:
                        c = PROJECT.index((kind, n))
                        act.wait_ge(p_product, NPC * s + c + 1)
                        src = PB[c % 2]
                        if kind == "ht":
                            nc.scalar.activation(h0t[:, 0, n, :], src[:, :], ACT.Relu).then_inc(p_high, 1)
                            continue
                        if attend:
                            act.wait_ge(scored, UNITS * a + 4 * n + 4)
                        for e in range(2):
                            own = slice(e * HD, (e + 1) * HD)
                            dst = q_st[own, n, e, :] if kind == "q" else k_st[own, n, e, 0, :]
                            bias = (bq if kind == "q" else bk)[own, n:n + 1]
                            ins = nc.scalar.activation(dst, src[own, :], ACT.Identity, bias=bias)
                        ins.then_inc(p_high, 1)
                    elif kind == "v" and project:
                        if attend:
                            need(act, summed, UNITS * a)
                        act.wait_ge(p_done, NPC * s + PROJECT.index(("v", n)) + 1)
                        nc.scalar.activation(v[:, odd, 0, n, :], v_sum[:, n % 2, :], ACT.Copy).then_inc(p_high, 1)
                    elif kind == "exp" and attend:
                        m, g, e = unit(n)
                        act.wait_ge(maxed, UNITS * a + n + 1)
                        need(act, transposed, UNITS * a + n - 1 if n else UNITS * a)
                        if n % 4 == 0:
                            need(act, normed, KT * a + m - 1 if m else KT * a)
                        for i in range(NT):
                            ins = nc.scalar.activation(probs[:, n % 2, i, :], masked[:, n % 2, i, :], ACT.Exp,
                                                       bias=neg_max[:, n % 2, i:i + 1], scale=-1.0,
                                                       accum_out=row_sum[:, m % 2, g * NT + i, e:e + 1])
                        ins.then_inc(exped, 1)
                    elif kind == "probs_t" and attend:
                        act.wait_ge(transposed, UNITS * a + n + 1)
                        need(act, summed, UNITS * a + n - 1 if n else UNITS * a)
                        nc.scalar.activation(probs_t[:, n % 2, 0, :, :], PT[:, :, :], ACT.Copy).then_inc(pt_high, 1)
                    elif kind in ("rht", "rq", "rv", "relt") and relate:
                        c = RELATE.index((kind, n))
                        act.wait_ge(r_product, NRC * l + c + 1)
                        dst = {"rht": h1t[:, 0, n % KT, :], "rq": rq[:, 0, n % KT, :], "rv": rv[:, 0, n % TILES, :],
                               "relt": rel_t[:, n % 2, 0, :, :].rearrange("p t n -> p (t n)")}[kind]
                        nc.scalar.activation(dst, RB[c % 2][:, :],
                                             ACT.Relu if kind == "rht" else ACT.Copy).then_inc(r_high, 1)
                    elif kind == "rel" and relate:
                        act.wait_ge(r_done, NRC * l + RELATE.index(("rel", n)) + 1)
                        for i in range(NT):
                            ins = nc.scalar.activation(squares[:, n, i, :], rel[:, n, i, :], ACT.Square,
                                                       accum_out=sq_sum[:, n, i:i + 1])
                        ins.then_inc(squared, 1)
                    elif kind == "ln0_apply" and ln0:
                        act.wait_ge(p_product, NPC * s + KT)
                        ln_apply(0, x_in[:, :, :], h0, s + 2)
                    elif kind == "ln1_apply" and attend:
                        if relate:
                            act.wait_ge(r_product, NRC * l + KT)
                        ln_apply(1, x_res[:, par, :, :], h1, a + 1)

            turns(act, turn, between)

        @block.vector
        def _(dve):
            def settle():
                dve.sem_inc(settled, 1)

            def refine(value, y, work, result_, done, steps, base):
                nc.vector.tensor_tensor(work, y, value, ALU.mult).then_inc(steps, 1)
                dve.wait_ge(steps, base + 1)
                nc.vector.tensor_tensor(work, work, y, ALU.mult).then_inc(steps, 1)
                dve.wait_ge(steps, base + 2)
                nc.vector.tensor_scalar(work, work, -0.5, 1.5, ALU.mult, ALU.add).then_inc(steps, 1)
                dve.wait_ge(steps, base + 3)
                nc.vector.tensor_tensor(result_, y, work, ALU.mult).then_inc(done, 1)

            LN_STEPS = 6

            def ln_stats(layer, src, count):
                base = LN_STEPS * (count - 1)
                for t in range(TILES):
                    ins = nc.vector.bn_stats(stats[:, layer, t, :], src[:, t, :])
                ins.then_inc(ln_steps[layer], 1)
                dve.wait_ge(ln_steps[layer], base + 1)
                settle()
                for t in range(TILES):
                    ins = nc.vector.bn_aggr(moments[:, layer, t, :], stats[:, layer, t, :])
                ins.then_inc(ln_steps[layer], 1)
                dve.wait_ge(ln_steps[layer], base + 2)
                nc.vector.tensor_scalar(var[:, layer, :], moments[:, layer, :, 1], EPS, None,
                                        ALU.add).then_inc(ln_var[layer], 1)

            def ln_scales(layer, count):
                base = LN_STEPS * (count - 1)
                dve.wait_ge(ln_guess[layer], count)
                refine(var[:, layer, :], guess[:, layer, :], ln_work[:, layer, :], rstd[:, layer, :],
                       ln_steps[layer], ln_steps[layer], base + 2)
                dve.wait_ge(ln_steps[layer], base + LN_STEPS)
                nc.vector.scalar_tensor_tensor(shift[:, layer, :], moments[:, layer, :, 0], -1.0,
                                               rstd[:, layer, :], ALU.mult, ALU.mult).then_inc(ln_scale[layer], 1)

            dve.wait_ge(x_loaded, 16)
            ln_stats(0, x_in[:, :, :], 1)
            stage = [x_res[:, 0, :, :], x_res[:, 1, :, :], h1[:, :, :]]
            for n, (w, scale) in enumerate(((wq, QS), (wk, WS), (wv, WS))):
                dve.wait_ge(w_high, n + 1)
                nc.vector.scalar_tensor_tensor(w[:, 1, :, :].rearrange("p t n -> p (t n)"),
                                               stage[n].rearrange("p t n -> p (t n)"), scale,
                                               w[:, 0, :, :].rearrange("p t n -> p (t n)"),
                                               ALU.mult, ALU.subtract).then_inc(w_low, 1)
                if n == 0:
                    ln_scales(0, 1)
            dve.wait_ge(small_loaded, 48)
            for b, scale in ((bq, QS), (bk, WS), (bv, WS)):
                ins = nc.vector.tensor_scalar(b[:, :], b[:, :], scale, None, ALU.mult)
            dve.wait_ge(adj_loaded, 16)
            nc.vector.tensor_scalar(mask[:, :, :], adj_in[:, :, :], 0.0, MASK,
                                    ALU.is_equal, ALU.mult).then_inc(scaled, 1)
            dve.wait_ge(scaled, 1)

            def between():
                for n in range(2 * KT):
                    dve.wait_ge(setup_high, n + 1)
                    w = (wm if n < KT else wvt)
                    nc.vector.scalar_tensor_tensor(w[:, 1, n % KT, :], S[n % 2][:, :, :].rearrange("p t n -> p (t n)"),
                                                   WS, w[:, 0, n % KT, :], ALU.mult, ALU.subtract).then_inc(setup_done, 1)
                dve.wait_ge(setup_product, 2 * KT + 1)
                nc.vector.tensor_copy(adj_t[:, :, :], S[0][:, :, :]).then_inc(setup_done, 1)

            def turn(s, odd):
                project, attend, relate, ln0, _ = stages(s, PAIRS)
                a, l = s - 1, s - 2
                par = 1 - odd
                for kind, n in PLAN:
                    if kind == "ht" and project:
                        c = PROJECT.index((kind, n))
                        dve.wait_ge(p_high, NPC * s + c + 1)
                        nc.vector.scalar_tensor_tensor(h0t[:, 1, n, :], PB[c % 2][:, :], 0.0, h0t[:, 0, n, :],
                                                       ALU.max, ALU.subtract).then_inc(p_done, 1)
                    elif kind in ("q", "k") and project:
                        c = PROJECT.index((kind, n))
                        dve.wait_ge(p_high, NPC * s + c + 1)
                        for e in range(2):
                            own, other = slice(e * HD, (e + 1) * HD), slice((1 - e) * HD, (2 - e) * HD)
                            if kind == "q":
                                hi, lo, b = q_st[own, n, e, :], q_st[other, n, e, :], bq
                            else:
                                hi, lo, b = k_st[own, n, e, 0, :], k_st[own, n, e, 1, :], bk
                            ins = nc.vector.scalar_tensor_tensor(lo, PB[c % 2][own, :], b[own, n:n + 1], hi,
                                                                 ALU.add, ALU.subtract)
                        ins.then_inc(p_done, 1)
                    elif kind == "v" and project:
                        c = PROJECT.index((kind, n))
                        dve.wait_ge(p_product, NPC * s + c + 1)
                        need(dve, v_low, TILES * s + n - 1 if n else TILES * s)
                        nc.vector.tensor_tensor(v_sum[:, n % 2, :], PB[c % 2][:, :], bv[:, :],
                                                ALU.add).then_inc(p_done, 1)
                    elif kind == "scores" and attend:
                        dve.wait_ge(scored, UNITS * a + n + 1)
                        need(dve, exped, UNITS * a + n - 1 if n else UNITS * a)
                        settle()
                        for i in range(NT):
                            ins = nc.vector.tensor_tensor_reduce(
                                out=masked[:, n % 2, i, :], in0=S[n % 2][:, i, :], in1=mask[:, i, :],
                                scale=SCORE, scalar=BIG, op0=ALU.add, op1=ALU.min,
                                accum_out=neg_max[:, n % 2, i:i + 1])
                        ins.then_inc(maxed, 1)
                    elif kind == "probs_t" and attend:
                        dve.wait_ge(pt_high, UNITS * a + n + 1)
                        nc.vector.tensor_tensor(probs_t[:, n % 2, 1, :, :], PT[:, :, :], probs_t[:, n % 2, 0, :, :],
                                                ALU.subtract).then_inc(pt_low, 1)
                    elif kind == "norm" and attend:
                        dve.wait_ge(summed, UNITS * a + 4 * n + 4)
                        nc.vector.reciprocal(row_inv[:, n % 2, :, :], row_sum[:, n % 2, :, :]).then_inc(inverted, 1)
                        dve.wait_ge(inverted, KT * a + n + 1)
                        need(dve, residual, KT * a + n - 1 if n else KT * a)
                        inv = row_inv[:, n % 2, :, :].rearrange("p t e -> p (t e)")
                        nc.vector.scalar_tensor_tensor(attn[:, n % 2, :, :], O[:, :, :], 1.0 / WS,
                                                       inv.unsqueeze(2).broadcast_to([P, TILES * 2, HD]),
                                                       ALU.mult, ALU.mult).then_inc(normed, 1)
                    elif kind in ("rht", "rq", "rv", "relt") and relate:
                        c = RELATE.index((kind, n))
                        dve.wait_ge(r_high, NRH * l + HALVED.index((kind, n)) + 1)
                        hi, lo = {"rht": (h1t[:, 0, n % KT, :], h1t[:, 1, n % KT, :]),
                                  "rq": (rq[:, 0, n % KT, :], rq[:, 1, n % KT, :]),
                                  "rv": (rv[:, 0, n % TILES, :], rv[:, 1, n % TILES, :]),
                                  "relt": (rel_t[:, n % 2, 0, :, :].rearrange("p t n -> p (t n)"),
                                           rel_t[:, n % 2, 1, :, :].rearrange("p t n -> p (t n)"))}[kind]
                        if kind == "rht":
                            nc.vector.scalar_tensor_tensor(lo, RB[c % 2][:, :], 0.0, hi,
                                                           ALU.max, ALU.subtract).then_inc(r_done, 1)
                        else:
                            nc.vector.tensor_tensor(lo, RB[c % 2][:, :], hi, ALU.subtract).then_inc(r_done, 1)
                    elif kind == "rel" and relate:
                        c = RELATE.index((kind, n))
                        dve.wait_ge(r_product, NRC * l + c + 1)
                        need(dve, rel_normed, 2 * l)
                        nc.vector.tensor_tensor(rel[:, n, :, :], RB[c % 2][:, :].rearrange("p (t n) -> p t n", t=NT),
                                                adj_t[:, :, :], ALU.mult).then_inc(r_done, 1)
                    elif kind == "out" and relate:
                        c = RELATE.index((kind, n))
                        dve.wait_ge(r_product, NRC * l + c + 1)
                        need(dve, stored[n % 2], 16 * (2 * l + n // 2))
                        nc.vector.scalar_tensor_tensor(result[:, n % 2, :], RB[c % 2][:, :], 1.0 / WS,
                                                       x_res[:, odd, n, :], ALU.mult, ALU.add).then_inc(r_done, 1)
                    elif kind == "rel_scale" and relate:
                        dve.wait_ge(rel_guess, 2 * l + n + 1)
                        refine(sq_sum[:, n, :], sq_pow[:, n, :], sq_work[:, :], rel_inv[:, n, :], rel_scale,
                               rel_steps, 6 * l + 3 * n)
                    elif kind == "ln0_stats" and ln0:
                        dve.wait_ge(x_loaded, 16 * (s + 2))
                        ln_stats(0, x_in[:, :, :], s + 2)
                    elif kind == "ln0_scale" and ln0:
                        ln_scales(0, s + 2)
                    elif kind == "ln1_stats" and attend:
                        dve.wait_ge(residual, KT * (a + 1))
                        ln_stats(1, x_res[:, par, :, :], a + 1)
                    elif kind == "ln1_scale" and attend:
                        ln_scales(1, a + 1)

            turns(dve, turn, between)

        @block.tensor
        def _(pe):
            def product(dst, left, right, pairs):
                for n, (i, j) in enumerate(pairs):
                    ins = nc.tensor.matmul(dst, left(i), right(j), start=(n == 0), stop=(n == len(pairs) - 1))
                return ins

            over_features = [((h1_, k), (h2_, k)) for k in range(KT) for h1_, h2_ in SPLIT]

            def col(n, size=P):
                return slice(n * size, (n + 1) * size)

            pe.wait_ge(consts_ready, 2)

            def between():
                for n in range(2 * KT + 1):
                    need(pe, setup_done, n - 1)
                    if n < KT:
                        if n == 0:
                            pe.wait_ge(w_loaded[3], 16)
                            pe.wait_ge(w_loaded[4], 16)
                        for k in range(KT):
                            ins = nc.tensor.matmul(S[n % 2][:, :, :].rearrange("p t n -> p (t n)"),
                                                   x_res[:, 0, k, col(n)], x_res[:, 1, k, :],
                                                   start=(k == 0), stop=(k == KT - 1))
                    elif n < 2 * KT:
                        if n == KT:
                            pe.wait_ge(w_loaded[5], 16)
                        flat = S[n % 2][:, :, :].rearrange("p t n -> p (t n)")
                        for k in range(KT):
                            ins = nc.tensor.transpose(flat[:, col(k)], h1[:, k, col(n - KT)], ident[:, :])
                    else:
                        pe.wait_ge(adj_loaded, 16)
                        for i in range(NT):
                            for j in range(NT):
                                ins = nc.tensor.transpose(S[0][:, i, col(j)], adj_in[:, j, col(i)], ident[:, :])
                    ins.then_inc(setup_product, 1)
                pe.wait_ge(setup_done, 2 * KT + 1)

            def turn(s, odd):
                project, attend, relate, _, _ = stages(s, PAIRS)
                a, l = s - 1, s - 2
                par = 1 - odd
                for kind, n in PLAN:
                    if kind in ("ht", "q", "k", "v") and project:
                        c = PROJECT.index((kind, n))
                        dst = PB[c % 2]
                        need(pe, p_done, NPC * s + c - 1)
                        if kind == "ht":
                            if n == 0:
                                pe.wait_ge(ln_done[0], s + 1)
                            for t in range(TILES):
                                ins = nc.tensor.transpose(dst[:, col(t)], h0[:, t, col(n)], ident[:, :])
                        elif kind == "v":
                            if n == 0:
                                if isinstance(s, int) and s == 0:
                                    pe.wait_ge(w_low, 3)
                                pe.wait_ge(p_done, NPC * s + KT)
                            ins = product(dst[:, :], lambda i: h0t[:, i[0], i[1], col(n)],
                                          lambda j: wv[:, j[0], j[1], :], over_features)
                        else:
                            w = wq if kind == "q" else wk
                            ins = product(dst[:, :], lambda i: w[:, i[0], i[1], col(n)],
                                          lambda j: h0t[:, j[0], j[1], :], over_features)
                        ins.then_inc(p_product, 1)
                    elif kind == "scores" and attend:
                        m, g, e = unit(n)
                        if n % 4 == 0:
                            pe.wait_ge(k_doubled[m], 32 * (a + 1))
                        need(pe, maxed, UNITS * a + n - 1 if n else UNITS * a)
                        for i in range(NT):
                            ins = product(S[n % 2][:, i, :], lambda _: q_st[:, m, e, col(g * NT + i)],
                                          lambda h: k_st[:, m, e, h, col(g, N)], [(0, 0), (0, 1)])
                        ins.then_inc(scored, 1)
                    elif kind == "probs_t" and attend:
                        pe.wait_ge(exped, UNITS * a + n + 1)
                        need(pe, pt_low, UNITS * a + n)
                        for i in range(NT):
                            for j in range(NT):
                                ins = nc.tensor.transpose(PT[:, j, col(i)], probs[:, n % 2, i, col(j)], ident[:, :])
                        ins.then_inc(transposed, 1)
                    elif kind == "pv" and attend:
                        m, g, e = unit(n)
                        if n == 0:
                            pe.wait_ge(v_low, TILES * (a + 1))
                        if n % 4 == 0:
                            need(pe, normed, KT * a + m)
                        pe.wait_ge(pt_low, UNITS * a + n + 1)
                        for i in range(NT):
                            ins = product(O[:, (g * NT + i) * 2 + e, :],
                                          lambda k: probs_t[:, n % 2, k[0], k[1], col(i)],
                                          lambda k: v[:, par, k[0], g * NT + k[1], col(2 * m + e, HD)],
                                          [((h1_, j), (h2_, j)) for j in range(NT) for h1_, h2_ in SPLIT])
                        ins.then_inc(summed, 1)
                    elif kind in ("rht", "rq", "rv", "rel", "relt", "out") and relate:
                        c = RELATE.index((kind, n))
                        dst = RB[c % 2]
                        need(pe, r_done, NRC * l + c - 1 if c else NRC * l)
                        if kind == "rht":
                            if n == 0:
                                pe.wait_ge(ln_done[1], l + 1)
                            for t in range(TILES):
                                ins = nc.tensor.transpose(dst[:, col(t)], h1[:, t, col(n)], ident[:, :])
                        elif kind == "rq":
                            if n == 0:
                                pe.wait_ge(r_done, NRC * l + KT)
                            ins = product(dst[:, :], lambda i: wm[:, i[0], i[1], col(n)],
                                          lambda j: h1t[:, j[0], j[1], :], over_features)
                        elif kind == "rv":
                            ins = product(dst[:, :], lambda i: h1t[:, i[0], i[1], col(n)],
                                          lambda j: wvt[:, j[0], j[1], :], over_features)
                        elif kind == "rel":
                            if n == 0:
                                pe.wait_ge(r_done, NRC * l + RELATE.index(("rq", KT - 1)) + 1)
                            for i in range(NT):
                                ins = product(dst[:, col(i, N)], lambda k: rq[:, k[0], k[1], col(n * NT + i)],
                                              lambda k: h1t[:, k[0], k[1], col(n, N)], over_features)
                        elif kind == "relt":
                            pe.wait_ge(rel_normed, 2 * l + n + 1)
                            for j in range(NT):
                                for i in range(NT):
                                    ins = nc.tensor.transpose(dst[:, j * N + i * P:j * N + (i + 1) * P],
                                                              rel_n[:, n, i, col(j)], ident[:, :])
                        else:
                            if n == 0:
                                pe.wait_ge(r_done, NRC * l + c)
                            g, i = n // NT, n % NT
                            ins = product(dst[:, :], lambda k: rel_t[:, g, k[0], k[1], col(i)],
                                          lambda k: rv[:, k[0], g * NT + k[1], :],
                                          [((h1_, j), (h2_, j)) for j in range(NT) for h1_, h2_ in SPLIT])
                        ins.then_inc(r_product, 1)

            turns(pe, turn, between)


_INS = ['x', 'adj', 'L0_gnn_Wq', 'L0_gnn_bq', 'L0_gnn_Wk', 'L0_gnn_bk', 'L0_gnn_Wv', 'L0_gnn_bv',
        'L1_gnn_Wq', 'L1_gnn_Wk', 'L1_gnn_Wv']


def kernel(**inputs):
    import numpy as _np
    import concourse.bacc as _bacc
    from concourse import mybir as _mybir
    from concourse.bass_utils import run_bass_kernel_spmd as _run

    nc = _bacc.Bacc("TRN2", target_bir_lowering=False, num_devices=1)
    arrays, args = {}, []
    for name in _INS:
        a = _np.ascontiguousarray(inputs[name])
        arrays[f"in_{name}_dram"] = a
        args.append(nc.dram_tensor(f"in_{name}_dram", a.shape, _mybir.dt.from_np(a.dtype), kind="ExternalInput").ap())
    shape = inputs['x'].shape
    args.append(nc.dram_tensor("out_0_dram", shape, _mybir.dt.float32, kind="ExternalOutput").ap())
    adjacency_attention_two_layers(nc, *args)
    r = _run(nc, [arrays], core_ids=[0])
    return r.results[0]["out_0_dram"]
```

```python
import concourse.bass as bass
from concourse import mybir
from contextlib import ExitStack


def adjacency_attention_two_layers(
    nc: bass.Bass,
    x: bass.AP,
    adj: bass.AP,
    wq0: bass.AP,
    bq0: bass.AP,
    wk0: bass.AP,
    bk0: bass.AP,
    wv0: bass.AP,
    bv0: bass.AP,
    wq1: bass.AP,
    wk1: bass.AP,
    wv1: bass.AP,
    out: bass.AP,
):
    fp32 = mybir.dt.float32
    fp16 = mybir.dt.float16
    ALU = mybir.AluOpType
    ACT = mybir.ActivationFunctionType

    GRAPHS, N, D = x.shape
    HEADS, HD = 8, 64
    P = 128
    PAIRS = GRAPHS // 2
    TOK = 2 * N
    TILES = TOK // P
    NT = N // P
    KT = D // P
    UNITS = 2 * HEADS
    EPS = 1e-5
    WS = 32.0
    QS = -WS * HD ** -0.5
    SCORE = -1.0 / (QS * WS * HD ** 0.5)
    MASK = 1.0e9 / SCORE
    SPLIT = ((0, 0), (0, 1), (1, 0))
    BIG = 3.0e38

    SLOTS = [("v", 0), ("v", 1), ("v", 2), ("v", 3), ("q", 0), ("rq", 0), ("k", 0), ("rq", 1),
             ("rq", 2), ("q", 1), ("rq", 3), ("k", 1), ("rv", 0), ("rel", 0), ("q", 2), ("rel", 1),
             ("rv", 1), ("k", 2), ("rv", 2), ("rv", 3), ("out", 0), ("q", 3), ("out", 1), ("out", 2),
             ("k", 3), ("out", 3)]
    BESIDE = {1: [("rht", 0)], 2: [("rht", 1)], 3: [("rht", 2)], 4: [("rht", 3)],
              7: [("ln0_stats", 0), ("ln0_stats", 1)], 8: [("ln0_stats", 2), ("ln0_stats", 3)],
              10: [("ln0_scale", 0), ("ln0_apply", 0)], 11: [("ln0_apply", 1)], 12: [("ln0_apply", 2)],
              13: [("ln0_apply", 3)], 14: [("squares", 0)], 15: [("rel_scale", 0), ("ht", 0)],
              16: [("squares", 1), ("ht", 1)],
              17: [("relt", 0), ("rel_scale", 1)], 18: [("ht", 2)], 19: [("relt", 1), ("ht", 3)],
              20: [("ln1_stats", 0), ("ln1_stats", 1)], 21: [("ln1_stats", 2), ("ln1_stats", 3)],
              23: [("ln1_scale", 0)], 24: [("ln1_apply", 0), ("ln1_apply", 1)],
              25: [("ln1_apply", 2), ("ln1_apply", 3)]}
    PLAN = [("turn", 0)]
    for at, big in enumerate(SLOTS):
        if at < UNITS:
            PLAN.append(("scores", at))
        if 0 <= at - 7 < UNITS and (at - 7) % 4 == 0:
            PLAN.append(("norm", (at - 7) // 4))
        if 0 <= at - 2 < UNITS:
            PLAN.append(("probs_t", at - 2))
        if at < UNITS:
            PLAN.append(("exp", at))
        PLAN += BESIDE.get(at, [])
        PLAN.append(big)
        if 0 <= at - 3 < UNITS:
            PLAN.append(("pv", at - 3))
    PROJECT = [st for st in PLAN if st[0] in ("ht", "q", "k", "v")]
    PROJECT_LAST = [st for st in PROJECT if st[0] != "ht"]
    RELATE = [st for st in PLAN if st[0] in ("rht", "rq", "rv", "rel", "relt", "out")]
    HALVED = [st for st in RELATE if st[0] in ("rht", "rq", "rv", "relt")]
    NPC, NRC, NRH = len(PROJECT), len(RELATE), len(HALVED)

    def before_project(s):
        return KT + NPC * s

    def in_project(step, ln0):
        return (PROJECT if ln0 else PROJECT_LAST).index(step)

    def unit(u):
        return u // 4, (u % 4) // 2, u % 2

    xv = x.rearrange("(n g) (t p) d -> n p (g t) d", g=2, p=P)
    ov = out.rearrange("(n g) (t p) d -> n p (g t) d", g=2, p=P)

    ctx = ExitStack()
    with ctx:
        def sb(name, shape, dt=fp32):
            return ctx.enter_context(nc.sbuf_tensor(name, shape, dt))

        def bank(name, shape):
            return ctx.enter_context(nc.psum_tensor(name, shape, fp32))

        def sem(name):
            return ctx.enter_context(nc.semaphore(name))

        wq = sb("wq", [P, 2, KT, D], fp16)
        wk = sb("wk", [P, 2, KT, D], fp16)
        wv = sb("wv", [P, 2, KT, D], fp16)
        wm = sb("wm", [P, 2, KT, D], fp16)
        wvt = sb("wvt", [P, 2, KT, D], fp16)
        bq = sb("bq", [P, KT])
        bk = sb("bk", [P, KT])
        bv = sb("bv", [P, D])
        ident = sb("ident", [P, P])
        adj_in = sb("adj_in", [P, NT, N])
        mask = sb("mask", [P, NT, N])
        adj_t = sb("adj_t", [P, NT, N])
        half = sb("half", [P, TILES])
        x_in = sb("x_in", [P, TILES, D])
        h = sb("h", [P, TILES, D])
        h0t = sb("h0t", [P, 2, 2, KT, TOK], fp16)
        q_st = sb("q_st", [P, KT, 2, TOK], fp16)
        k_st = sb("k_st", [P, KT, 2, 2, TOK], fp16)
        v_sum = sb("v_sum", [P, 2, D])
        v = sb("v", [P, 2, 2, TILES, D], fp16)
        x_res = sb("x_res", [P, 2, TILES, D])
        masked = sb("masked", [P, 2, NT, N])
        neg_max = sb("neg_max", [P, 2, NT])
        probs = sb("probs", [P, 2, NT, N])
        row_sum = sb("row_sum", [P, 2, TILES, 2])
        row_inv = sb("row_inv", [P, 2, TILES, 2])
        probs_t = sb("probs_t", [P, 2, 2, NT, N], fp16)
        attn = sb("attn", [P, 2, TILES * 2, HD])
        h1t = sb("h1t", [P, 2, KT, TOK], fp16)
        rq = sb("rq", [P, 2, KT, TOK], fp16)
        rv = sb("rv", [P, 2, TILES, D], fp16)
        rel = sb("rel", [P, 2, NT, N])
        rel_n = sb("rel_n", [P, 2, NT, N])
        rel_t = sb("rel_t", [P, 2, 2, NT, N], fp16)
        sq_sum = sb("sq_sum", [P, 2, NT])
        sq_pow = sb("sq_pow", [P, 2, NT])
        sq_work = sb("sq_work", [P, NT])
        rel_inv = sb("rel_inv", [P, 2, NT])
        result = sb("result", [P, 2, D])
        stats = sb("stats", [P, 2, TILES, 6])
        moments = sb("moments", [P, 2, TILES, 2])
        var = sb("var", [P, 2, TILES])
        guess = sb("guess", [P, 2, TILES])
        ln_work = sb("ln_work", [P, 2, TILES])
        rstd = sb("rstd", [P, 2, TILES])
        shift = sb("shift", [P, 2, TILES])

        S = [bank(f"S{i}", [P, NT, N]) for i in range(2)]
        PT = bank("PT", [P, NT, N])
        O = bank("O", [P, TILES * 2, HD])
        PB = [bank(f"PB{i}", [P, TOK]) for i in range(2)]
        RB = [bank(f"RB{i}", [P, TOK]) for i in range(2)]

        x_loaded = sem("x_loaded")
        res_loaded = [sem(f"res_loaded{i}") for i in range(2)]
        w_loaded = [sem(f"w_loaded{i}") for i in range(6)]
        small_loaded = sem("small_loaded")
        adj_loaded = sem("adj_loaded")
        k_doubled = [sem(f"k_doubled{m}") for m in range(KT)]
        stored = [sem(f"stored{i}") for i in range(2)]
        consts_ready = sem("consts_ready")
        ident_zero = sem("ident_zero")
        w_high = sem("w_high")
        w_low = sem("w_low")
        scaled = sem("scaled")
        setup_product = sem("setup_product")
        setup_high = sem("setup_high")
        setup_done = sem("setup_done")
        p_product = sem("p_product")
        p_high = sem("p_high")
        p_done = sem("p_done")
        v_low = sem("v_low")
        scored = sem("scored")
        maxed = sem("maxed")
        exped = sem("exped")
        transposed = sem("transposed")
        pt_high = sem("pt_high")
        pt_low = sem("pt_low")
        summed = sem("summed")
        inverted = sem("inverted")
        normed = sem("normed")
        residual = sem("residual")
        settled = sem("settled")
        r_product = sem("r_product")
        r_high = sem("r_high")
        r_done = sem("r_done")
        squared = sem("squared")
        rel_guess = sem("rel_guess")
        rel_steps = sem("rel_steps")
        rel_scale = sem("rel_scale")
        rel_normed = sem("rel_normed")
        ln_steps = [sem(f"ln_steps{i}") for i in range(2)]
        ln_var = [sem(f"ln_var{i}") for i in range(2)]
        ln_guess = [sem(f"ln_guess{i}") for i in range(2)]
        ln_scale = [sem(f"ln_scale{i}") for i in range(2)]
        ln_done = [sem(f"ln_done{i}") for i in range(2)]

        block = ctx.enter_context(nc.Block())

        stage = [x_res[:, 0, :, :], x_res[:, 1, :, :],
                 rq[:, :, :, :].rearrange("p a k t -> p (a k t)").bitcast(fp32).rearrange("p (k t) -> p k t", k=KT)]

        def need(eng, semaphore, value):
            if not (isinstance(value, int) and value <= 0):
                eng.wait_ge(semaphore, value)

        def stages(s, last):
            if not isinstance(s, int):
                return True, True, True, True, True
            return s < last, 1 <= s <= last, s >= 2, s + 1 < last, s + 2 < last

        def turns(eng, turn, between):
            turn(0, 0)
            between()
            for s in range(1, 4):
                turn(s, s % 2)
            with eng.Fori(0, (PAIRS - 6) // 2) as i:
                for odd in range(2):
                    turn(2 * i + 4 + odd, odd)
            for s in range(PAIRS - 2, PAIRS + 2):
                turn(s, s % 2)

        @block.sync
        def _(sp):
            sp.dma_start(x_in[:, :, :], xv[0]).then_inc(x_loaded, 16)
            for n, w in enumerate((wq0, wk0, wv0)):
                sp.dma_start(stage[n], w.rearrange("(t p) n -> p t n", p=P)).then_inc(w_loaded[n], 16)
            sp.dma_start(adj_in[:, :, :], adj.rearrange("(t p) n -> p t n", p=P)).then_inc(adj_loaded, 16)
            for n, w in enumerate((wq1, wk1, wv1)):
                sp.wait_ge(w_low, n + 1)
                sp.dma_start(stage[n], w.rearrange("(t p) n -> p t n", p=P)).then_inc(w_loaded[3 + n], 16)
            sp.wait_ge(ln_done[0], TILES)
            sp.dma_start(x_in[:, :, :], xv[1]).then_inc(x_loaded, 16)

            def between():
                sp.wait_ge(setup_done, 2 * KT + 1)

            def turn(s, odd):
                project, attend, relate, ln0, load = stages(s, PAIRS)
                a, l = s - 1, s - 2
                par = 1 - odd
                for kind, n in PLAN:
                    if kind == "turn" and attend:
                        if relate:
                            need(sp, r_done, NRC * l)
                        sp.dma_start(x_res[:, par, :, :], xv[a]).then_inc(res_loaded[par], 16)
                    elif kind == "k" and project:
                        sp.wait_ge(p_done, before_project(s) + in_project((kind, n), ln0) + 1)
                        for e in range(2):
                            own, other = slice(e * HD, (e + 1) * HD), slice((1 - e) * HD, (2 - e) * HD)
                            sp.dma_start(k_st[other, n, e, :, :], k_st[own, n, e, :, :]).then_inc(k_doubled[n], 16)
                    elif (kind, n) == ("ln0_apply", TILES - 1) and load:
                        sp.wait_ge(ln_done[0], TILES * (s + 2))
                        sp.dma_start(x_in[:, :, :], xv[s + 2]).then_inc(x_loaded, 16)
                    elif kind == "out" and relate:
                        sp.wait_ge(r_done, NRC * l + RELATE.index(("out", n)) + 1)
                        sp.dma_start(ov[l][:, n, :], result[:, n % 2, :]).then_inc(stored[n % 2], 16)

            turns(sp, turn, between)
            for i in range(2):
                sp.wait_ge(stored[i], 16 * PAIRS * TILES // 2)

        @block.gpsimd
        def _(pool):
            nc.gpsimd.memset(ident[:, :], 0.0).then_inc(ident_zero, 1)
            nc.gpsimd.memset(half[:, :], -0.5).then_inc(consts_ready, 1)
            pool.wait_ge(ident_zero, 1)
            nc.gpsimd.affine_select(out=ident[:, :], in_=ident[:, :], compare_op=ALU.not_equal, fill=1.0,
                                    base=0, pattern=[[-1, P]], channel_multiplier=1).then_inc(consts_ready, 1)
            pool.wait_ge(consts_ready, 2)

            def ln_power(layer, count):
                pool.wait_ge(ln_var[layer], count)
                nc.gpsimd.tensor_tensor(guess[:, layer, :], var[:, layer, :], half[:, :],
                                        ALU.pow).then_inc(ln_guess[layer], 1)

            ln_power(0, 1)

            def turn(s, odd):
                project, attend, relate, ln0, _ = stages(s, PAIRS)
                a, l = s - 1, s - 2
                par = 1 - odd
                for kind, n in PLAN:
                    if kind == "v" and project:
                        pool.wait_ge(p_high, before_project(s) + in_project((kind, n), ln0) + 1)
                        nc.gpsimd.tensor_tensor(v[:, odd, 1, n, :], v_sum[:, n % 2, :], v[:, odd, 0, n, :],
                                                ALU.subtract).then_inc(v_low, 1)
                    elif kind == "ln0_scale" and ln0:
                        ln_power(0, s + 2)
                    elif kind == "ln1_scale" and attend:
                        ln_power(1, a + 1)
                    elif kind == "norm" and attend:
                        if n == 0:
                            pool.wait_ge(res_loaded[par], 8 * (a - par) + 16)
                        pool.wait_ge(normed, KT * a + n + 1)
                        cols = x_res[:, par, :, n * P:(n + 1) * P]
                        nc.gpsimd.tensor_tensor(cols, cols,
                                                attn[:, n % 2, :, :].rearrange("p (t e) d -> p t (e d)", e=2),
                                                ALU.add).then_inc(residual, 1)
                    elif kind == "squares" and relate:
                        pool.wait_ge(squared, 2 * l + n + 1)
                        nc.gpsimd.tensor_tensor(sq_pow[:, n, :], sq_sum[:, n, :], half[:, 0:NT],
                                                ALU.pow).then_inc(rel_guess, 1)
                    elif kind == "rel_scale" and relate:
                        pool.wait_ge(rel_scale, 2 * l + n + 1)
                        nc.gpsimd.tensor_tensor(rel_n[:, n, :, :], rel[:, n, :, :],
                                                rel_inv[:, n, :].unsqueeze(2).broadcast_to([P, NT, N]),
                                                ALU.mult).then_inc(rel_normed, 1)

            turns(pool, turn, lambda: None)

        @block.scalar
        def _(act):
            act.dma_start(bq[:, :], bq0.rearrange("(m p) -> p m", p=P),
                          allow_slow_non_contiguous=True).then_inc(small_loaded, 16)
            act.dma_start(bk[:, :], bk0.rearrange("(m p) -> p m", p=P),
                          allow_slow_non_contiguous=True).then_inc(small_loaded, 16)
            act.dma_start(bv[:, :], bv0.partition_broadcast(P)).then_inc(small_loaded, 16)

            for n, (w, scale) in enumerate(((wq, QS), (wk, WS), (wv, WS))):
                act.wait_ge(w_loaded[n], 16)
                nc.scalar.activation(w[:, 0, :, :], stage[n], ACT.Copy, scale=scale).then_inc(w_high, 1)

            def ln_apply(layer, src, t, count):
                act.wait_ge(ln_scale[layer], count)
                nc.scalar.activation(h[:, t, :], src[:, t, :], ACT.Identity, scale=rstd[:, layer, t:t + 1],
                                     bias=shift[:, layer, t:t + 1]).then_inc(ln_done[layer], 1)

            def h0t_high(parity, n, chunk, bank_):
                act.wait_ge(p_product, chunk + 1)
                nc.scalar.activation(h0t[:, parity, 0, n, :], bank_[:, :], ACT.Relu).then_inc(p_high, 1)

            for t in range(TILES):
                ln_apply(0, x_in, t, 1)
            for n in range(KT):
                h0t_high(0, n, n, PB[n % 2])
            act.wait_ge(scaled, 1)

            def between():
                for n in range(2 * KT):
                    act.wait_ge(setup_product, n + 1)
                    dst = (wm if n < KT else wvt)[:, 0, n % KT, :]
                    nc.scalar.activation(dst, S[n % 2][:, :, :], ACT.Copy, scale=WS).then_inc(setup_high, 1)

            def turn(s, odd):
                project, attend, relate, ln0, _ = stages(s, PAIRS)
                a, l = s - 1, s - 2
                par = 1 - odd
                for kind, n in PLAN:
                    if kind == "ht" and ln0:
                        c = in_project((kind, n), ln0)
                        h0t_high(1 - odd, n, before_project(s) + c, PB[c % 2])
                    elif kind in ("q", "k") and project:
                        c = in_project((kind, n), ln0)
                        act.wait_ge(p_product, before_project(s) + c + 1)
                        src = PB[c % 2]
                        if attend:
                            act.wait_ge(scored, UNITS * a + 4 * n + 4)
                        for e in range(2):
                            own = slice(e * HD, (e + 1) * HD)
                            dst = q_st[own, n, e, :] if kind == "q" else k_st[own, n, e, 0, :]
                            bias = (bq if kind == "q" else bk)[own, n:n + 1]
                            ins = nc.scalar.activation(dst, src[own, :], ACT.Identity, bias=bias)
                        ins.then_inc(p_high, 1)
                    elif kind == "v" and project:
                        if attend:
                            need(act, summed, UNITS * a)
                        act.wait_ge(p_done, before_project(s) + in_project((kind, n), ln0) + 1)
                        nc.scalar.activation(v[:, odd, 0, n, :], v_sum[:, n % 2, :], ACT.Copy).then_inc(p_high, 1)
                    elif kind == "exp" and attend:
                        m, g, e = unit(n)
                        act.wait_ge(maxed, UNITS * a + n + 1)
                        need(act, transposed, UNITS * a + n - 1)
                        if n % 4 == 0:
                            need(act, normed, KT * a + m - 1)
                        for i in range(NT):
                            ins = nc.scalar.activation(probs[:, n % 2, i, :], masked[:, n % 2, i, :], ACT.Exp,
                                                       bias=neg_max[:, n % 2, i:i + 1], scale=-1.0,
                                                       accum_out=row_sum[:, m % 2, g * NT + i, e:e + 1])
                        ins.then_inc(exped, 1)
                    elif kind == "probs_t" and attend:
                        act.wait_ge(transposed, UNITS * a + n + 1)
                        need(act, summed, UNITS * a + n - 1)
                        nc.scalar.activation(probs_t[:, n % 2, 0, :, :], PT[:, :, :], ACT.Copy).then_inc(pt_high, 1)
                    elif kind in ("rht", "rq", "rv", "relt") and relate:
                        c = RELATE.index((kind, n))
                        act.wait_ge(r_product, NRC * l + c + 1)
                        dst = {"rht": h1t[:, 0, n % KT, :], "rq": rq[:, 0, n % KT, :], "rv": rv[:, 0, n % TILES, :],
                               "relt": rel_t[:, n % 2, 0, :, :].rearrange("p t n -> p (t n)")}[kind]
                        nc.scalar.activation(dst, RB[c % 2][:, :],
                                             ACT.Relu if kind == "rht" else ACT.Copy).then_inc(r_high, 1)
                    elif kind == "squares" and relate:
                        act.wait_ge(r_done, NRC * l + RELATE.index(("rel", n)) + 1)
                        need(act, r_product, NRC * l)
                        for i in range(NT):
                            ins = nc.scalar.activation(rel_n[:, n, i, :], rel[:, n, i, :], ACT.Square,
                                                       accum_out=sq_sum[:, n, i:i + 1])
                        ins.then_inc(squared, 1)
                    elif kind == "ln0_apply" and ln0:
                        ln_apply(0, x_in, n, s + 2)
                    elif kind == "ln1_apply" and attend:
                        ln_apply(1, x_res[:, par, :, :], n, a + 1)

            turns(act, turn, between)

        @block.vector
        def _(dve):
            def settle():
                dve.sem_inc(settled, 1)

            def refine(value, y, work, result_, done, steps, base):
                nc.vector.tensor_tensor(work, y, value, ALU.mult).then_inc(steps, 1)
                dve.wait_ge(steps, base + 1)
                nc.vector.tensor_tensor(work, work, y, ALU.mult).then_inc(steps, 1)
                dve.wait_ge(steps, base + 2)
                nc.vector.tensor_scalar(work, work, -0.5, 1.5, ALU.mult, ALU.add).then_inc(steps, 1)
                dve.wait_ge(steps, base + 3)
                nc.vector.tensor_tensor(result_, y, work, ALU.mult).then_inc(done, 1)

            LN_STEPS = 6

            def ln_stats(layer, src, t, count):
                base = LN_STEPS * (count - 1)
                ins = nc.vector.bn_stats(stats[:, layer, t, :], src[:, t, :])
                if t < TILES - 1:
                    return
                ins.then_inc(ln_steps[layer], 1)
                dve.wait_ge(ln_steps[layer], base + 1)
                settle()
                for t in range(TILES):
                    ins = nc.vector.bn_aggr(moments[:, layer, t, :], stats[:, layer, t, :])
                ins.then_inc(ln_steps[layer], 1)
                dve.wait_ge(ln_steps[layer], base + 2)
                nc.vector.tensor_scalar(var[:, layer, :], moments[:, layer, :, 1], EPS, None,
                                        ALU.add).then_inc(ln_var[layer], 1)

            def ln_scales(layer, count):
                base = LN_STEPS * (count - 1)
                dve.wait_ge(ln_guess[layer], count)
                refine(var[:, layer, :], guess[:, layer, :], ln_work[:, layer, :], rstd[:, layer, :],
                       ln_steps[layer], ln_steps[layer], base + 2)
                dve.wait_ge(ln_steps[layer], base + LN_STEPS)
                nc.vector.scalar_tensor_tensor(shift[:, layer, :], moments[:, layer, :, 0], -1.0,
                                               rstd[:, layer, :], ALU.mult, ALU.mult).then_inc(ln_scale[layer], 1)

            def h0t_low(parity, n, chunk, bank_):
                dve.wait_ge(p_high, chunk + 1)
                nc.vector.scalar_tensor_tensor(h0t[:, parity, 1, n, :], bank_[:, :], 0.0, h0t[:, parity, 0, n, :],
                                               ALU.max, ALU.subtract).then_inc(p_done, 1)

            dve.wait_ge(x_loaded, 16)
            for t in range(TILES):
                ln_stats(0, x_in, t, 1)
            for n, (w, scale) in enumerate(((wq, QS), (wk, WS), (wv, WS))):
                dve.wait_ge(w_high, n + 1)
                nc.vector.scalar_tensor_tensor(w[:, 1, :, :].rearrange("p t n -> p (t n)"),
                                               stage[n].rearrange("p t n -> p (t n)"), scale,
                                               w[:, 0, :, :].rearrange("p t n -> p (t n)"),
                                               ALU.mult, ALU.subtract).then_inc(w_low, 1)
                if n == 0:
                    ln_scales(0, 1)
            for n in range(KT):
                h0t_low(0, n, n, PB[n % 2])
            dve.wait_ge(small_loaded, 48)
            for b, scale in ((bq, QS), (bk, WS), (bv, WS)):
                ins = nc.vector.tensor_scalar(b[:, :], b[:, :], scale, None, ALU.mult)
            dve.wait_ge(adj_loaded, 16)
            nc.vector.tensor_scalar(mask[:, :, :], adj_in[:, :, :], 0.0, MASK,
                                    ALU.is_equal, ALU.mult).then_inc(scaled, 1)
            dve.wait_ge(scaled, 1)

            def between():
                for n in range(2 * KT):
                    dve.wait_ge(setup_high, n + 1)
                    w = (wm if n < KT else wvt)
                    nc.vector.scalar_tensor_tensor(w[:, 1, n % KT, :], S[n % 2][:, :, :].rearrange("p t n -> p (t n)"),
                                                   WS, w[:, 0, n % KT, :], ALU.mult, ALU.subtract).then_inc(setup_done, 1)
                dve.wait_ge(setup_product, 2 * KT + 1)
                nc.vector.tensor_copy(adj_t[:, :, :], S[0][:, :, :]).then_inc(setup_done, 1)

            def turn(s, odd):
                project, attend, relate, ln0, _ = stages(s, PAIRS)
                a, l = s - 1, s - 2
                par = 1 - odd
                for kind, n in PLAN:
                    if kind == "ht" and ln0:
                        c = in_project((kind, n), ln0)
                        h0t_low(1 - odd, n, before_project(s) + c, PB[c % 2])
                    elif kind in ("q", "k") and project:
                        c = in_project((kind, n), ln0)
                        dve.wait_ge(p_high, before_project(s) + c + 1)
                        for e in range(2):
                            own, other = slice(e * HD, (e + 1) * HD), slice((1 - e) * HD, (2 - e) * HD)
                            if kind == "q":
                                hi, lo, b = q_st[own, n, e, :], q_st[other, n, e, :], bq
                            else:
                                hi, lo, b = k_st[own, n, e, 0, :], k_st[own, n, e, 1, :], bk
                            ins = nc.vector.scalar_tensor_tensor(lo, PB[c % 2][own, :], b[own, n:n + 1], hi,
                                                                 ALU.add, ALU.subtract)
                        ins.then_inc(p_done, 1)
                    elif kind == "v" and project:
                        c = in_project((kind, n), ln0)
                        dve.wait_ge(p_product, before_project(s) + c + 1)
                        need(dve, v_low, TILES * s + n - 1)
                        nc.vector.tensor_tensor(v_sum[:, n % 2, :], PB[c % 2][:, :], bv[:, :],
                                                ALU.add).then_inc(p_done, 1)
                    elif kind == "scores" and attend:
                        dve.wait_ge(scored, UNITS * a + n + 1)
                        need(dve, exped, UNITS * a + n - 1)
                        settle()
                        for i in range(NT):
                            ins = nc.vector.tensor_tensor_reduce(
                                out=masked[:, n % 2, i, :], in0=S[n % 2][:, i, :], in1=mask[:, i, :],
                                scale=SCORE, scalar=BIG, op0=ALU.add, op1=ALU.min,
                                accum_out=neg_max[:, n % 2, i:i + 1])
                        ins.then_inc(maxed, 1)
                    elif kind == "probs_t" and attend:
                        dve.wait_ge(pt_high, UNITS * a + n + 1)
                        nc.vector.tensor_tensor(probs_t[:, n % 2, 1, :, :], PT[:, :, :], probs_t[:, n % 2, 0, :, :],
                                                ALU.subtract).then_inc(pt_low, 1)
                    elif kind == "norm" and attend:
                        dve.wait_ge(summed, UNITS * a + 4 * n + 4)
                        nc.vector.reciprocal(row_inv[:, n % 2, :, :], row_sum[:, n % 2, :, :]).then_inc(inverted, 1)
                        dve.wait_ge(inverted, KT * a + n + 1)
                        need(dve, residual, KT * a + n - 1)
                        inv = row_inv[:, n % 2, :, :].rearrange("p t e -> p (t e)")
                        nc.vector.scalar_tensor_tensor(attn[:, n % 2, :, :], O[:, :, :], 1.0 / WS,
                                                       inv.unsqueeze(2).broadcast_to([P, TILES * 2, HD]),
                                                       ALU.mult, ALU.mult).then_inc(normed, 1)
                    elif kind in ("rht", "rq", "rv", "relt") and relate:
                        c = RELATE.index((kind, n))
                        dve.wait_ge(r_high, NRH * l + HALVED.index((kind, n)) + 1)
                        hi, lo = {"rht": (h1t[:, 0, n % KT, :], h1t[:, 1, n % KT, :]),
                                  "rq": (rq[:, 0, n % KT, :], rq[:, 1, n % KT, :]),
                                  "rv": (rv[:, 0, n % TILES, :], rv[:, 1, n % TILES, :]),
                                  "relt": (rel_t[:, n % 2, 0, :, :].rearrange("p t n -> p (t n)"),
                                           rel_t[:, n % 2, 1, :, :].rearrange("p t n -> p (t n)"))}[kind]
                        if kind == "rht":
                            nc.vector.scalar_tensor_tensor(lo, RB[c % 2][:, :], 0.0, hi,
                                                           ALU.max, ALU.subtract).then_inc(r_done, 1)
                        else:
                            nc.vector.tensor_tensor(lo, RB[c % 2][:, :], hi, ALU.subtract).then_inc(r_done, 1)
                    elif kind == "rel" and relate:
                        c = RELATE.index((kind, n))
                        dve.wait_ge(r_product, NRC * l + c + 1)
                        need(dve, rel_normed, 2 * l)
                        nc.vector.tensor_tensor(rel[:, n, :, :], RB[c % 2][:, :].rearrange("p (t n) -> p t n", t=NT),
                                                adj_t[:, :, :], ALU.mult).then_inc(r_done, 1)
                    elif kind == "out" and relate:
                        c = RELATE.index((kind, n))
                        dve.wait_ge(r_product, NRC * l + c + 1)
                        need(dve, stored[n % 2], 16 * (2 * l + n // 2))
                        nc.vector.scalar_tensor_tensor(result[:, n % 2, :], RB[c % 2][:, :], 1.0 / WS,
                                                       x_res[:, odd, n, :], ALU.mult, ALU.add).then_inc(r_done, 1)
                    elif kind == "rel_scale" and relate:
                        dve.wait_ge(rel_guess, 2 * l + n + 1)
                        refine(sq_sum[:, n, :], sq_pow[:, n, :], sq_work[:, :], rel_inv[:, n, :], rel_scale,
                               rel_steps, 6 * l + 3 * n)
                    elif kind == "ln0_stats" and ln0:
                        if n == 0:
                            dve.wait_ge(x_loaded, 16 * (s + 2))
                        ln_stats(0, x_in, n, s + 2)
                    elif kind == "ln0_scale" and ln0:
                        ln_scales(0, s + 2)
                    elif kind == "ln1_stats" and attend:
                        if n == 0:
                            dve.wait_ge(residual, KT * (a + 1))
                        ln_stats(1, x_res[:, par, :, :], n, a + 1)
                    elif kind == "ln1_scale" and attend:
                        ln_scales(1, a + 1)

            turns(dve, turn, between)

        @block.tensor
        def _(pe):
            def product(dst, left, right, pairs):
                for n, (i, j) in enumerate(pairs):
                    ins = nc.tensor.matmul(dst, left(i), right(j), start=(n == 0), stop=(n == len(pairs) - 1))
                return ins

            over_features = [((h1_, k), (h2_, k)) for k in range(KT) for h1_, h2_ in SPLIT]

            def col(n, size=P):
                return slice(n * size, (n + 1) * size)

            def h_transposed(n, dst):
                for t in range(TILES):
                    ins = nc.tensor.transpose(dst[:, col(t)], h[:, t, col(n)], ident[:, :])
                return ins

            pe.wait_ge(consts_ready, 2)
            pe.wait_ge(ln_done[0], TILES)
            for n in range(KT):
                need(pe, p_done, n - 1)
                h_transposed(n, PB[n % 2]).then_inc(p_product, 1)

            def between():
                for n in range(2 * KT + 1):
                    need(pe, setup_done, n - 1)
                    if n < KT:
                        if n == 0:
                            pe.wait_ge(w_loaded[3], 16)
                            pe.wait_ge(w_loaded[4], 16)
                        for k in range(KT):
                            ins = nc.tensor.matmul(S[n % 2][:, :, :].rearrange("p t n -> p (t n)"),
                                                   stage[0][:, k, col(n)], stage[1][:, k, :],
                                                   start=(k == 0), stop=(k == KT - 1))
                    elif n < 2 * KT:
                        if n == KT:
                            pe.wait_ge(w_loaded[5], 16)
                        flat = S[n % 2][:, :, :].rearrange("p t n -> p (t n)")
                        for k in range(KT):
                            ins = nc.tensor.transpose(flat[:, col(k)], stage[2][:, k, col(n - KT)], ident[:, :])
                    else:
                        pe.wait_ge(adj_loaded, 16)
                        for i in range(NT):
                            for j in range(NT):
                                ins = nc.tensor.transpose(S[0][:, i, col(j)], adj_in[:, j, col(i)], ident[:, :])
                    ins.then_inc(setup_product, 1)
                pe.wait_ge(setup_done, 2 * KT + 1)

            def turn(s, odd):
                project, attend, relate, ln0, _ = stages(s, PAIRS)
                a, l = s - 1, s - 2
                par = 1 - odd
                for kind, n in PLAN:
                    if (kind in ("q", "k", "v") and project) or (kind == "ht" and ln0):
                        c = in_project((kind, n), ln0)
                        dst = PB[c % 2]
                        need(pe, p_done, before_project(s) + c - 1)
                        if kind == "ht":
                            if n == 0:
                                pe.wait_ge(ln_done[0], TILES * (s + 2))
                            ins = h_transposed(n, dst)
                        elif kind == "v":
                            if n == 0:
                                first = isinstance(s, int) and s == 0
                                if first:
                                    pe.wait_ge(w_low, 3)
                                pe.wait_ge(p_done, KT if first else
                                           before_project(s - 1) + PROJECT.index(("ht", KT - 1)) + 1)
                            ins = product(dst[:, :], lambda i: h0t[:, odd, i[0], i[1], col(n)],
                                          lambda j: wv[:, j[0], j[1], :], over_features)
                        else:
                            w = wq if kind == "q" else wk
                            ins = product(dst[:, :], lambda i: w[:, i[0], i[1], col(n)],
                                          lambda j: h0t[:, odd, j[0], j[1], :], over_features)
                        ins.then_inc(p_product, 1)
                    elif kind == "scores" and attend:
                        m, g, e = unit(n)
                        if n % 4 == 0:
                            pe.wait_ge(k_doubled[m], 32 * (a + 1))
                        need(pe, maxed, UNITS * a + n - 1)
                        for i in range(NT):
                            ins = product(S[n % 2][:, i, :], lambda _: q_st[:, m, e, col(g * NT + i)],
                                          lambda h: k_st[:, m, e, h, col(g, N)], [(0, 0), (0, 1)])
                        ins.then_inc(scored, 1)
                    elif kind == "probs_t" and attend:
                        pe.wait_ge(exped, UNITS * a + n + 1)
                        need(pe, pt_low, UNITS * a + n)
                        for i in range(NT):
                            for j in range(NT):
                                ins = nc.tensor.transpose(PT[:, j, col(i)], probs[:, n % 2, i, col(j)], ident[:, :])
                        ins.then_inc(transposed, 1)
                    elif kind == "pv" and attend:
                        m, g, e = unit(n)
                        if n == 0:
                            pe.wait_ge(v_low, TILES * (a + 1))
                        if n % 4 == 0:
                            need(pe, normed, KT * a + m)
                        pe.wait_ge(pt_low, UNITS * a + n + 1)
                        for i in range(NT):
                            ins = product(O[:, (g * NT + i) * 2 + e, :],
                                          lambda k: probs_t[:, n % 2, k[0], k[1], col(i)],
                                          lambda k: v[:, par, k[0], g * NT + k[1], col(2 * m + e, HD)],
                                          [((h1_, j), (h2_, j)) for j in range(NT) for h1_, h2_ in SPLIT])
                        ins.then_inc(summed, 1)
                    elif kind in ("rht", "rq", "rv", "rel", "relt", "out") and relate:
                        c = RELATE.index((kind, n))
                        dst = RB[c % 2]
                        need(pe, r_done, NRC * l + c - 1)
                        if kind == "rht":
                            if n == 0:
                                pe.wait_ge(ln_done[1], TILES * (l + 1))
                            ins = h_transposed(n, dst)
                        elif kind == "rq":
                            if n == 0:
                                pe.wait_ge(r_done, NRC * l + RELATE.index(("rht", KT - 1)) + 1)
                            ins = product(dst[:, :], lambda i: wm[:, i[0], i[1], col(n)],
                                          lambda j: h1t[:, j[0], j[1], :], over_features)
                        elif kind == "rv":
                            ins = product(dst[:, :], lambda i: h1t[:, i[0], i[1], col(n)],
                                          lambda j: wvt[:, j[0], j[1], :], over_features)
                        elif kind == "rel":
                            if n == 0:
                                pe.wait_ge(r_done, NRC * l + RELATE.index(("rq", KT - 1)) + 1)
                            for i in range(NT):
                                ins = product(dst[:, col(i, N)], lambda k: rq[:, k[0], k[1], col(n * NT + i)],
                                              lambda k: h1t[:, k[0], k[1], col(n, N)], over_features)
                        elif kind == "relt":
                            pe.wait_ge(rel_normed, 2 * l + n + 1)
                            for j in range(NT):
                                for i in range(NT):
                                    ins = nc.tensor.transpose(dst[:, j * N + i * P:j * N + (i + 1) * P],
                                                              rel_n[:, n, i, col(j)], ident[:, :])
                        else:
                            g, i = n // NT, n % NT
                            if i == 0:
                                pe.wait_ge(r_done, NRC * l + 1 + max(RELATE.index(("relt", g)),
                                                                     RELATE.index(("rv", g * NT + NT - 1))))
                            ins = product(dst[:, :], lambda k: rel_t[:, g, k[0], k[1], col(i)],
                                          lambda k: rv[:, k[0], g * NT + k[1], :],
                                          [((h1_, j), (h2_, j)) for j in range(NT) for h1_, h2_ in SPLIT])
                        ins.then_inc(r_product, 1)

            turns(pe, turn, between)


_INS = ['x', 'adj', 'L0_gnn_Wq', 'L0_gnn_bq', 'L0_gnn_Wk', 'L0_gnn_bk', 'L0_gnn_Wv', 'L0_gnn_bv',
        'L1_gnn_Wq', 'L1_gnn_Wk', 'L1_gnn_Wv']


def kernel(**inputs):
    import numpy as _np
    import concourse.bacc as _bacc
    from concourse import mybir as _mybir
    from concourse.bass_utils import run_bass_kernel_spmd as _run

    nc = _bacc.Bacc("TRN2", target_bir_lowering=False, num_devices=1)
    arrays, args = {}, []
    for name in _INS:
        a = _np.ascontiguousarray(inputs[name])
        arrays[f"in_{name}_dram"] = a
        args.append(nc.dram_tensor(f"in_{name}_dram", a.shape, _mybir.dt.from_np(a.dtype), kind="ExternalInput").ap())
    shape = inputs['x'].shape
    args.append(nc.dram_tensor("out_0_dram", shape, _mybir.dt.float32, kind="ExternalOutput").ap())
    adjacency_attention_two_layers(nc, *args)
    r = _run(nc, [arrays], core_ids=[0])
    return r.results[0]["out_0_dram"]
```

```python
import concourse.bass as bass
from concourse import mybir
from contextlib import ExitStack


def adjacency_attention_two_layers(
    nc: bass.Bass,
    x: bass.AP,
    adj: bass.AP,
    wq0: bass.AP,
    bq0: bass.AP,
    wk0: bass.AP,
    bk0: bass.AP,
    wv0: bass.AP,
    bv0: bass.AP,
    wq1: bass.AP,
    wk1: bass.AP,
    wv1: bass.AP,
    out: bass.AP,
):
    fp32 = mybir.dt.float32
    fp16 = mybir.dt.float16
    ALU = mybir.AluOpType
    ACT = mybir.ActivationFunctionType

    GRAPHS, N, D = x.shape
    HEADS, HD = 8, 64
    P = 128
    PAIRS = GRAPHS // 2
    TOK = 2 * N
    TILES = TOK // P
    NT = N // P
    KT = D // P
    UNITS = 2 * HEADS
    EPS = 1e-5
    WS = 32.0
    QS = -WS * HD ** -0.5
    SCORE = -1.0 / (QS * WS * HD ** 0.5)
    MASK = 1.0e9 / SCORE
    SPLIT = ((0, 0), (0, 1), (1, 0))
    BIG = 3.0e38

    SLOTS = [("v", 0), ("v", 1), ("v", 2), ("v", 3), ("q", 0), ("rq", 0), ("k", 0), ("rq", 1),
             ("rq", 2), ("q", 1), ("rq", 3), ("k", 1), ("rv", 0), ("rel", 0), ("q", 2), ("rel", 1),
             ("rv", 1), ("k", 2), ("rv", 2), ("rv", 3), ("out", 0), ("q", 3), ("out", 1), ("out", 2),
             ("k", 3), ("out", 3)]
    BESIDE = {1: [("rht", 0)], 2: [("rht", 1)], 3: [("rht", 2)], 4: [("rht", 3)],
              7: [("ln0_stats", 0), ("ln0_stats", 1)], 8: [("ln0_stats", 2), ("ln0_stats", 3)],
              10: [("ln0_scale", 0), ("ln0_apply", 0)], 11: [("ln0_apply", 1)], 12: [("ln0_apply", 2)],
              13: [("ln0_apply", 3)], 14: [("squares", 0)], 15: [("rel_scale", 0), ("ht", 0)],
              16: [("squares", 1), ("ht", 1)],
              17: [("relt", 0), ("rel_scale", 1)], 18: [("ht", 2)], 19: [("relt", 1), ("ht", 3)],
              20: [("ln1_stats", 0), ("ln1_stats", 1)], 21: [("ln1_stats", 2), ("ln1_stats", 3)],
              23: [("ln1_scale", 0)], 24: [("ln1_apply", 0), ("ln1_apply", 1)],
              25: [("ln1_apply", 2), ("ln1_apply", 3)]}

    def slot(at, big):
        steps = []
        if (at - 7) in range(0, UNITS, 4):
            steps.append(("norm", (at - 7) // 4))
        if at < UNITS:
            steps.append(("scores", at))
        if at - 2 in range(UNITS):
            steps.append(("probs_t", at - 2))
        steps += BESIDE.get(at, [])
        if (at - 5) in range(0, UNITS, 4):
            steps.append(("inverse", (at - 5) // 4))
        steps.append(big)
        if at < UNITS:
            steps.append(("exp", at))
        if at - 3 in range(UNITS):
            steps.append(("pv", at - 3))
        return steps

    PLAN = [("turn", 0)] + [step for at, big in enumerate(SLOTS) for step in slot(at, big)]
    PROJECT = [st for st in PLAN if st[0] in ("ht", "q", "k", "v")]
    PROJECT_LAST = [st for st in PROJECT if st[0] != "ht"]
    RELATE = [st for st in PLAN if st[0] in ("rht", "rq", "rv", "rel", "relt", "out")]
    HALVED = [st for st in RELATE if st[0] in ("rht", "rq", "rv", "relt")]
    NPC, NRC, NRH = len(PROJECT), len(RELATE), len(HALVED)

    SETUP = [st for st in RELATE if st[0] in ("rq", "rv") or st == ("rel", 0)]
    NSETUP = len(SETUP)

    def before_project(s):
        return KT + NPC * s

    def in_project(step, ln0):
        return (PROJECT if ln0 else PROJECT_LAST).index(step)

    def unit(u):
        return u // 4, (u % 4) // 2, u % 2

    xv = x.rearrange("(n g) (t p) d -> n p (g t) d", g=2, p=P)
    ov = out.rearrange("(n g) (t p) d -> n p (g t) d", g=2, p=P)

    ctx = ExitStack()
    with ctx:
        def sb(name, shape, dt=fp32):
            return ctx.enter_context(nc.sbuf_tensor(name, shape, dt))

        def bank(name, shape):
            return ctx.enter_context(nc.psum_tensor(name, shape, fp32))

        def sem(name):
            return ctx.enter_context(nc.semaphore(name))

        wq = sb("wq", [P, 2, KT, D], fp16)
        wk = sb("wk", [P, 2, KT, D], fp16)
        wv = sb("wv", [P, 2, KT, D], fp16)
        wm = sb("wm", [P, 2, KT, D], fp16)
        wvt = sb("wvt", [P, 2, KT, D], fp16)
        bq = sb("bq", [P, KT])
        bk = sb("bk", [P, KT])
        bv = sb("bv", [P, D])
        ident = sb("ident", [P, P])
        adj_in = sb("adj_in", [P, NT, N])
        mask = sb("mask", [P, NT, N])
        adj_t = sb("adj_t", [P, NT, N])
        half = sb("half", [P, TILES])
        x_in = sb("x_in", [P, TILES, D])
        h = sb("h", [P, TILES, D])
        h0t = sb("h0t", [P, 2, 2, KT, TOK], fp16)
        q_st = sb("q_st", [P, KT, 2, TOK], fp16)
        k_st = sb("k_st", [P, KT, 2, 2, TOK], fp16)
        v_sum = sb("v_sum", [P, 2, D])
        v = sb("v", [P, 2, 2, TILES, D], fp16)
        x_res = sb("x_res", [P, 2, TILES, D])
        masked = sb("masked", [P, 2, NT, N])
        neg_max = sb("neg_max", [P, 2, NT])
        probs = sb("probs", [P, 4, NT, N])
        row_sum = sb("row_sum", [P, 2, TILES, 2])
        row_inv = sb("row_inv", [P, 2, TILES, 2])
        probs_t = sb("probs_t", [P, 2, 2, NT, N], fp16)
        attn = sb("attn", [P, 2, TILES * 2, HD])
        h1t = sb("h1t", [P, 2, KT, TOK], fp16)
        rq = sb("rq", [P, 2, KT, TOK], fp16)
        rv = sb("rv", [P, 2, TILES, D], fp16)
        rel = sb("rel", [P, 2, NT, N])
        rel_n = sb("rel_n", [P, 2, NT, N])
        rel_t = sb("rel_t", [P, 2, 2, NT, N], fp16)
        sq_sum = sb("sq_sum", [P, 2, NT])
        sq_pow = sb("sq_pow", [P, 2, NT])
        sq_work = sb("sq_work", [P, NT])
        rel_inv = sb("rel_inv", [P, 2, NT])
        result = sb("result", [P, 2, D])
        stats = sb("stats", [P, 2, TILES, 6])
        moments = sb("moments", [P, 2, TILES, 2])
        var = sb("var", [P, 2, TILES])
        guess = sb("guess", [P, 2, TILES])
        ln_work = sb("ln_work", [P, 2, TILES])
        rstd = sb("rstd", [P, 2, TILES])
        shift = sb("shift", [P, 2, TILES])

        S = [bank(f"S{i}", [P, NT, N]) for i in range(2)]
        PT = bank("PT", [P, NT, N])
        O = bank("O", [P, TILES * 2, HD])
        PB = [bank(f"PB{i}", [P, TOK]) for i in range(2)]
        RB = [bank(f"RB{i}", [P, TOK]) for i in range(2)]

        x_loaded = sem("x_loaded")
        res_loaded = [sem(f"res_loaded{i}") for i in range(2)]
        w_loaded = [sem(f"w_loaded{i}") for i in range(6)]
        small_loaded = sem("small_loaded")
        adj_loaded = sem("adj_loaded")
        k_doubled = [sem(f"k_doubled{m}") for m in range(KT)]
        stored = [sem(f"stored{i}") for i in range(2)]
        consts_ready = sem("consts_ready")
        ident_zero = sem("ident_zero")
        w_high = sem("w_high")
        w_low = sem("w_low")
        scaled = sem("scaled")
        setup_product = sem("setup_product")
        setup_high = sem("setup_high")
        setup_done = sem("setup_done")
        p_product = sem("p_product")
        p_high = sem("p_high")
        p_done = sem("p_done")
        v_low = sem("v_low")
        scored = sem("scored")
        maxed = sem("maxed")
        exped = sem("exped")
        transposed = sem("transposed")
        pt_high = sem("pt_high")
        pt_low = sem("pt_low")
        summed = sem("summed")
        inverted = sem("inverted")
        normed = sem("normed")
        residual = sem("residual")
        settled = sem("settled")
        r_product = sem("r_product")
        r_high = sem("r_high")
        r_done = sem("r_done")
        squared = sem("squared")
        rel_guess = sem("rel_guess")
        rel_steps = sem("rel_steps")
        rel_scale = sem("rel_scale")
        rel_normed = sem("rel_normed")
        ln_steps = [sem(f"ln_steps{i}") for i in range(2)]
        ln_var = [sem(f"ln_var{i}") for i in range(2)]
        ln_guess = [sem(f"ln_guess{i}") for i in range(2)]
        ln_scale = [sem(f"ln_scale{i}") for i in range(2)]
        ln_done = [sem(f"ln_done{i}") for i in range(2)]

        block = ctx.enter_context(nc.Block())

        def as_weight(buffer):
            return buffer[:, :, :, :].rearrange("p a k t -> p (a k t)").bitcast(fp32)\
                                     .rearrange("p (k t) -> p k t", k=KT)

        stage = [as_weight(rv), as_weight(rq), x_res[:, 1, :, :]]

        def need(eng, semaphore, value):
            if not (isinstance(value, int) and value <= 0):
                eng.wait_ge(semaphore, value)

        def stages(s, last):
            if not isinstance(s, int):
                return True, True, True, True, True
            return s < last, 1 <= s <= last, s >= 2, s + 1 < last, s + 2 < last

        def turns(eng, turn):
            for s in range(4):
                turn(s, s % 2)
            with eng.Fori(0, (PAIRS - 6) // 2) as i:
                for odd in range(2):
                    turn(2 * i + 4 + odd, odd)
            for s in range(PAIRS - 2, PAIRS + 2):
                turn(s, s % 2)

        @block.sync
        def _(sp):
            sp.dma_start(x_in[:, :, :], xv[0]).then_inc(x_loaded, 16)
            for n, w in enumerate((wv0, wq0, wk0)):
                sp.dma_start(stage[n], w.rearrange("(t p) n -> p t n", p=P)).then_inc(w_loaded[n], 16)
            sp.dma_start(adj_in[:, :, :], adj.rearrange("(t p) n -> p t n", p=P)).then_inc(adj_loaded, 16)
            for n, w in enumerate((wv1, wq1, wk1)):
                sp.wait_ge(w_low, n + 1)
                sp.dma_start(stage[n], w.rearrange("(t p) n -> p t n", p=P)).then_inc(w_loaded[3 + n], 16)
            sp.wait_ge(ln_done[0], TILES)
            sp.dma_start(x_in[:, :, :], xv[1]).then_inc(x_loaded, 16)

            def turn(s, odd):
                project, attend, relate, ln0, load = stages(s, PAIRS)
                a, l = s - 1, s - 2
                par = 1 - odd
                for kind, n in PLAN:
                    if kind == "turn" and attend:
                        if isinstance(s, int) and s == 2:
                            sp.wait_ge(setup_done, NSETUP)
                        if relate:
                            need(sp, r_done, NRC * l)
                        sp.dma_start(x_res[:, par, :, :], xv[a]).then_inc(res_loaded[par], 16)
                    elif kind == "k" and project:
                        sp.wait_ge(p_done, before_project(s) + in_project((kind, n), ln0) + 1)
                        for e in range(2):
                            own, other = slice(e * HD, (e + 1) * HD), slice((1 - e) * HD, (2 - e) * HD)
                            sp.dma_start(k_st[other, n, e, :, :], k_st[own, n, e, :, :]).then_inc(k_doubled[n], 16)
                    elif (kind, n) == ("ln0_apply", TILES - 1) and load:
                        sp.wait_ge(ln_done[0], TILES * (s + 2))
                        sp.dma_start(x_in[:, :, :], xv[s + 2]).then_inc(x_loaded, 16)
                    elif kind == "out" and relate:
                        sp.wait_ge(r_done, NRC * l + RELATE.index(("out", n)) + 1)
                        sp.dma_start(ov[l][:, n, :], result[:, n % 2, :]).then_inc(stored[n % 2], 16)

            turns(sp, turn)
            for i in range(2):
                sp.wait_ge(stored[i], 16 * PAIRS * TILES // 2)

        @block.gpsimd
        def _(pool):
            nc.gpsimd.memset(ident[:, :], 0.0).then_inc(ident_zero, 1)
            nc.gpsimd.memset(half[:, :], -0.5).then_inc(consts_ready, 1)
            pool.wait_ge(ident_zero, 1)
            nc.gpsimd.affine_select(out=ident[:, :], in_=ident[:, :], compare_op=ALU.not_equal, fill=1.0,
                                    base=0, pattern=[[-1, P]], channel_multiplier=1).then_inc(consts_ready, 1)
            pool.wait_ge(consts_ready, 2)

            def ln_power(layer, count):
                pool.wait_ge(ln_var[layer], count)
                nc.gpsimd.tensor_tensor(guess[:, layer, :], var[:, layer, :], half[:, :],
                                        ALU.pow).then_inc(ln_guess[layer], 1)

            ln_power(0, 1)

            def turn(s, odd):
                project, attend, relate, ln0, _ = stages(s, PAIRS)
                a, l = s - 1, s - 2
                par = 1 - odd
                for kind, n in PLAN:
                    if kind == "v" and project:
                        pool.wait_ge(p_high, before_project(s) + in_project((kind, n), ln0) + 1)
                        nc.gpsimd.tensor_tensor(v[:, odd, 1, n, :], v_sum[:, n % 2, :], v[:, odd, 0, n, :],
                                                ALU.subtract).then_inc(v_low, 1)
                    elif kind == "ln0_scale" and ln0:
                        ln_power(0, s + 2)
                    elif kind == "ln1_scale" and attend:
                        ln_power(1, a + 1)
                    elif kind == "norm" and attend:
                        if n == 0:
                            pool.wait_ge(res_loaded[par], 8 * (a - par) + 16)
                        pool.wait_ge(normed, KT * a + n + 1)
                        cols = x_res[:, par, :, n * P:(n + 1) * P]
                        nc.gpsimd.tensor_tensor(cols, cols,
                                                attn[:, n % 2, :, :].rearrange("p (t e) d -> p t (e d)", e=2),
                                                ALU.add).then_inc(residual, 1)
                    elif kind == "squares" and relate:
                        pool.wait_ge(squared, 2 * l + n + 1)
                        nc.gpsimd.tensor_tensor(sq_pow[:, n, :], sq_sum[:, n, :], half[:, 0:NT],
                                                ALU.pow).then_inc(rel_guess, 1)
                    elif kind == "rel_scale" and relate:
                        pool.wait_ge(rel_scale, 2 * l + n + 1)
                        nc.gpsimd.tensor_tensor(rel_n[:, n, :, :], rel[:, n, :, :],
                                                rel_inv[:, n, :].unsqueeze(2).broadcast_to([P, NT, N]),
                                                ALU.mult).then_inc(rel_normed, 1)

            turns(pool, turn)

        @block.scalar
        def _(act):
            act.dma_start(bq[:, :], bq0.rearrange("(m p) -> p m", p=P),
                          allow_slow_non_contiguous=True).then_inc(small_loaded, 16)
            act.dma_start(bk[:, :], bk0.rearrange("(m p) -> p m", p=P),
                          allow_slow_non_contiguous=True).then_inc(small_loaded, 16)
            act.dma_start(bv[:, :], bv0.partition_broadcast(P)).then_inc(small_loaded, 16)

            def ln_apply(layer, src, t, count):
                act.wait_ge(ln_scale[layer], count)
                nc.scalar.activation(h[:, t, :], src[:, t, :], ACT.Identity, scale=rstd[:, layer, t:t + 1],
                                     bias=shift[:, layer, t:t + 1]).then_inc(ln_done[layer], 1)

            def h0t_high(parity, n, chunk, bank_):
                act.wait_ge(p_product, chunk + 1)
                nc.scalar.activation(h0t[:, parity, 0, n, :], bank_[:, :], ACT.Relu).then_inc(p_high, 1)

            for t in range(TILES):
                ln_apply(0, x_in, t, 1)
            for n, (w, scale) in enumerate(((wv, WS), (wq, QS), (wk, WS))):
                if n == 1:
                    for c in range(KT):
                        h0t_high(0, c, c, PB[c % 2])
                act.wait_ge(w_loaded[n], 16)
                nc.scalar.activation(w[:, 0, :, :], stage[n], ACT.Copy, scale=scale).then_inc(w_high, 1)
            act.wait_ge(scaled, 1)

            def setup_high_half(step):
                kind, n = step
                c = SETUP.index(step)
                if kind != "rel":
                    act.wait_ge(setup_product, c + 1)
                    dst = (wm if kind == "rq" else wvt)[:, 0, n, :]
                    nc.scalar.activation(dst, RB[c % 2][:, :], ACT.Copy, scale=WS).then_inc(setup_high, 1)

            def turn(s, odd):
                project, attend, relate, ln0, _ = stages(s, PAIRS)
                a, l = s - 1, s - 2
                par = 1 - odd
                for kind, n in PLAN:
                    if kind == "ht" and ln0:
                        c = in_project((kind, n), ln0)
                        h0t_high(1 - odd, n, before_project(s) + c, PB[c % 2])
                    elif kind in ("q", "k") and project:
                        c = in_project((kind, n), ln0)
                        act.wait_ge(p_product, before_project(s) + c + 1)
                        src = PB[c % 2]
                        if attend:
                            act.wait_ge(scored, UNITS * a + 4 * n + 4)
                        for e in range(2):
                            own = slice(e * HD, (e + 1) * HD)
                            dst = q_st[own, n, e, :] if kind == "q" else k_st[own, n, e, 0, :]
                            bias = (bq if kind == "q" else bk)[own, n:n + 1]
                            ins = nc.scalar.activation(dst, src[own, :], ACT.Identity, bias=bias)
                        ins.then_inc(p_high, 1)
                    elif kind == "v" and project:
                        if attend:
                            need(act, summed, UNITS * a)
                        act.wait_ge(p_done, before_project(s) + in_project((kind, n), ln0) + 1)
                        nc.scalar.activation(v[:, odd, 0, n, :], v_sum[:, n % 2, :], ACT.Copy).then_inc(p_high, 1)
                    elif kind == "exp" and attend:
                        m, g, e = unit(n)
                        act.wait_ge(maxed, UNITS * a + n + 1)
                        need(act, transposed, UNITS * a + n - 3)
                        if n % 4 == 0:
                            need(act, inverted, KT * a + m - 1)
                        for i in range(NT):
                            ins = nc.scalar.activation(probs[:, n % 4, i, :], masked[:, n % 2, i, :], ACT.Exp,
                                                       bias=neg_max[:, n % 2, i:i + 1], scale=-1.0,
                                                       accum_out=row_sum[:, m % 2, g * NT + i, e:e + 1])
                        ins.then_inc(exped, 1)
                    elif kind == "probs_t" and attend:
                        act.wait_ge(transposed, UNITS * a + n + 1)
                        need(act, summed, UNITS * a + n - 1)
                        nc.scalar.activation(probs_t[:, n % 2, 0, :, :], PT[:, :, :], ACT.Copy).then_inc(pt_high, 1)
                    elif (kind, n) in SETUP and isinstance(s, int) and s == 1:
                        setup_high_half((kind, n))
                    elif kind in ("rht", "rq", "rv", "relt") and relate:
                        c = RELATE.index((kind, n))
                        act.wait_ge(r_product, NRC * l + c + 1)
                        dst = {"rht": h1t[:, 0, n % KT, :], "rq": rq[:, 0, n % KT, :], "rv": rv[:, 0, n % TILES, :],
                               "relt": rel_t[:, n % 2, 0, :, :].rearrange("p t n -> p (t n)")}[kind]
                        nc.scalar.activation(dst, RB[c % 2][:, :],
                                             ACT.Relu if kind == "rht" else ACT.Copy).then_inc(r_high, 1)
                    elif kind == "squares" and relate:
                        act.wait_ge(r_done, NRC * l + RELATE.index(("rel", n)) + 1)
                        need(act, r_product, NRC * l)
                        for i in range(NT):
                            ins = nc.scalar.activation(rel_n[:, n, i, :], rel[:, n, i, :], ACT.Square,
                                                       accum_out=sq_sum[:, n, i:i + 1])
                        ins.then_inc(squared, 1)
                    elif kind == "ln0_apply" and ln0:
                        ln_apply(0, x_in, n, s + 2)
                    elif kind == "ln1_apply" and attend:
                        ln_apply(1, x_res[:, par, :, :], n, a + 1)

            turns(act, turn)

        @block.vector
        def _(dve):
            def settle():
                dve.sem_inc(settled, 1)

            def refine(value, y, work, result_, done, steps, base):
                nc.vector.tensor_tensor(work, y, value, ALU.mult).then_inc(steps, 1)
                dve.wait_ge(steps, base + 1)
                nc.vector.tensor_tensor(work, work, y, ALU.mult).then_inc(steps, 1)
                dve.wait_ge(steps, base + 2)
                nc.vector.tensor_scalar(work, work, -0.5, 1.5, ALU.mult, ALU.add).then_inc(steps, 1)
                dve.wait_ge(steps, base + 3)
                nc.vector.tensor_tensor(result_, y, work, ALU.mult).then_inc(done, 1)

            LN_STEPS = 6

            def ln_stats(layer, src, t, count):
                base = LN_STEPS * (count - 1)
                ins = nc.vector.bn_stats(stats[:, layer, t, :], src[:, t, :])
                if t < TILES - 1:
                    return
                ins.then_inc(ln_steps[layer], 1)
                dve.wait_ge(ln_steps[layer], base + 1)
                settle()
                for t in range(TILES):
                    ins = nc.vector.bn_aggr(moments[:, layer, t, :], stats[:, layer, t, :])
                ins.then_inc(ln_steps[layer], 1)
                dve.wait_ge(ln_steps[layer], base + 2)
                nc.vector.tensor_scalar(var[:, layer, :], moments[:, layer, :, 1], EPS, None,
                                        ALU.add).then_inc(ln_var[layer], 1)

            def ln_scales(layer, count):
                base = LN_STEPS * (count - 1)
                dve.wait_ge(ln_guess[layer], count)
                refine(var[:, layer, :], guess[:, layer, :], ln_work[:, layer, :], rstd[:, layer, :],
                       ln_steps[layer], ln_steps[layer], base + 2)
                dve.wait_ge(ln_steps[layer], base + LN_STEPS)
                nc.vector.scalar_tensor_tensor(shift[:, layer, :], moments[:, layer, :, 0], -1.0,
                                               rstd[:, layer, :], ALU.mult, ALU.mult).then_inc(ln_scale[layer], 1)

            def h0t_low(parity, n, chunk, bank_):
                dve.wait_ge(p_high, chunk + 1)
                nc.vector.scalar_tensor_tensor(h0t[:, parity, 1, n, :], bank_[:, :], 0.0, h0t[:, parity, 0, n, :],
                                               ALU.max, ALU.subtract).then_inc(p_done, 1)

            dve.wait_ge(x_loaded, 16)
            for t in range(TILES):
                ln_stats(0, x_in, t, 1)
            ln_scales(0, 1)
            for n, (w, scale) in enumerate(((wv, WS), (wq, QS), (wk, WS))):
                if n == 1:
                    for c in range(KT):
                        h0t_low(0, c, c, PB[c % 2])
                dve.wait_ge(w_high, n + 1)
                nc.vector.scalar_tensor_tensor(w[:, 1, :, :].rearrange("p t n -> p (t n)"),
                                               stage[n].rearrange("p t n -> p (t n)"), scale,
                                               w[:, 0, :, :].rearrange("p t n -> p (t n)"),
                                               ALU.mult, ALU.subtract).then_inc(w_low, 1)
            dve.wait_ge(small_loaded, 48)
            for b, scale in ((bq, QS), (bk, WS), (bv, WS)):
                ins = nc.vector.tensor_scalar(b[:, :], b[:, :], scale, None, ALU.mult)
            dve.wait_ge(adj_loaded, 16)
            nc.vector.tensor_scalar(mask[:, :, :], adj_in[:, :, :], 0.0, MASK,
                                    ALU.is_equal, ALU.mult).then_inc(scaled, 1)
            dve.wait_ge(scaled, 1)

            def setup_low_half(step):
                kind, n = step
                c = SETUP.index(step)
                if kind == "rel":
                    dve.wait_ge(setup_product, c + 1)
                    nc.vector.tensor_copy(adj_t[:, :, :].rearrange("p t n -> p (t n)"),
                                          RB[c % 2][:, :]).then_inc(setup_done, 1)
                else:
                    dve.wait_ge(setup_high, c + 1 - (c > SETUP.index(("rel", 0))))
                    w = wm if kind == "rq" else wvt
                    nc.vector.scalar_tensor_tensor(w[:, 1, n, :], RB[c % 2][:, :], WS, w[:, 0, n, :],
                                                   ALU.mult, ALU.subtract).then_inc(setup_done, 1)

            def turn(s, odd):
                project, attend, relate, ln0, _ = stages(s, PAIRS)
                a, l = s - 1, s - 2
                par = 1 - odd
                for kind, n in PLAN:
                    if kind == "ht" and ln0:
                        c = in_project((kind, n), ln0)
                        h0t_low(1 - odd, n, before_project(s) + c, PB[c % 2])
                    elif kind in ("q", "k") and project:
                        c = in_project((kind, n), ln0)
                        dve.wait_ge(p_high, before_project(s) + c + 1)
                        for e in range(2):
                            own, other = slice(e * HD, (e + 1) * HD), slice((1 - e) * HD, (2 - e) * HD)
                            if kind == "q":
                                hi, lo, b = q_st[own, n, e, :], q_st[other, n, e, :], bq
                            else:
                                hi, lo, b = k_st[own, n, e, 0, :], k_st[own, n, e, 1, :], bk
                            ins = nc.vector.scalar_tensor_tensor(lo, PB[c % 2][own, :], b[own, n:n + 1], hi,
                                                                 ALU.add, ALU.subtract)
                        ins.then_inc(p_done, 1)
                    elif kind == "v" and project:
                        c = in_project((kind, n), ln0)
                        dve.wait_ge(p_product, before_project(s) + c + 1)
                        need(dve, v_low, TILES * s + n - 1)
                        nc.vector.tensor_tensor(v_sum[:, n % 2, :], PB[c % 2][:, :], bv[:, :],
                                                ALU.add).then_inc(p_done, 1)
                    elif kind == "scores" and attend:
                        dve.wait_ge(scored, UNITS * a + n + 1)
                        need(dve, exped, UNITS * a + n - 1)
                        settle()
                        for i in range(NT):
                            ins = nc.vector.tensor_tensor_reduce(
                                out=masked[:, n % 2, i, :], in0=S[n % 2][:, i, :], in1=mask[:, i, :],
                                scale=SCORE, scalar=BIG, op0=ALU.add, op1=ALU.min,
                                accum_out=neg_max[:, n % 2, i:i + 1])
                        ins.then_inc(maxed, 1)
                    elif kind == "probs_t" and attend:
                        dve.wait_ge(pt_high, UNITS * a + n + 1)
                        nc.vector.tensor_tensor(probs_t[:, n % 2, 1, :, :], PT[:, :, :], probs_t[:, n % 2, 0, :, :],
                                                ALU.subtract).then_inc(pt_low, 1)
                    elif kind == "inverse" and attend:
                        dve.wait_ge(exped, UNITS * a + 4 * n + 4)
                        nc.vector.reciprocal(row_inv[:, n % 2, :, :], row_sum[:, n % 2, :, :]).then_inc(inverted, 1)
                    elif kind == "norm" and attend:
                        dve.wait_ge(summed, UNITS * a + 4 * n + 4)
                        dve.wait_ge(inverted, KT * a + n + 1)
                        need(dve, residual, KT * a + n - 1)
                        inv = row_inv[:, n % 2, :, :].rearrange("p t e -> p (t e)")
                        nc.vector.scalar_tensor_tensor(attn[:, n % 2, :, :], O[:, :, :], 1.0 / WS,
                                                       inv.unsqueeze(2).broadcast_to([P, TILES * 2, HD]),
                                                       ALU.mult, ALU.mult).then_inc(normed, 1)
                    elif (kind, n) in SETUP and isinstance(s, int) and s == 1:
                        setup_low_half((kind, n))
                    elif kind in ("rht", "rq", "rv", "relt") and relate:
                        c = RELATE.index((kind, n))
                        dve.wait_ge(r_high, NRH * l + HALVED.index((kind, n)) + 1)
                        hi, lo = {"rht": (h1t[:, 0, n % KT, :], h1t[:, 1, n % KT, :]),
                                  "rq": (rq[:, 0, n % KT, :], rq[:, 1, n % KT, :]),
                                  "rv": (rv[:, 0, n % TILES, :], rv[:, 1, n % TILES, :]),
                                  "relt": (rel_t[:, n % 2, 0, :, :].rearrange("p t n -> p (t n)"),
                                           rel_t[:, n % 2, 1, :, :].rearrange("p t n -> p (t n)"))}[kind]
                        if kind == "rht":
                            nc.vector.scalar_tensor_tensor(lo, RB[c % 2][:, :], 0.0, hi,
                                                           ALU.max, ALU.subtract).then_inc(r_done, 1)
                        else:
                            nc.vector.tensor_tensor(lo, RB[c % 2][:, :], hi, ALU.subtract).then_inc(r_done, 1)
                    elif kind == "rel" and relate:
                        c = RELATE.index((kind, n))
                        dve.wait_ge(r_product, NRC * l + c + 1)
                        need(dve, rel_normed, 2 * l)
                        nc.vector.tensor_tensor(rel[:, n, :, :], RB[c % 2][:, :].rearrange("p (t n) -> p t n", t=NT),
                                                adj_t[:, :, :], ALU.mult).then_inc(r_done, 1)
                    elif kind == "out" and relate:
                        c = RELATE.index((kind, n))
                        dve.wait_ge(r_product, NRC * l + c + 1)
                        need(dve, stored[n % 2], 16 * (2 * l + n // 2))
                        nc.vector.scalar_tensor_tensor(result[:, n % 2, :], RB[c % 2][:, :], 1.0 / WS,
                                                       x_res[:, odd, n, :], ALU.mult, ALU.add).then_inc(r_done, 1)
                    elif kind == "rel_scale" and relate:
                        dve.wait_ge(rel_guess, 2 * l + n + 1)
                        refine(sq_sum[:, n, :], sq_pow[:, n, :], sq_work[:, :], rel_inv[:, n, :], rel_scale,
                               rel_steps, 6 * l + 3 * n)
                    elif kind == "ln0_stats" and ln0:
                        if n == 0:
                            dve.wait_ge(x_loaded, 16 * (s + 2))
                        ln_stats(0, x_in, n, s + 2)
                    elif kind == "ln0_scale" and ln0:
                        ln_scales(0, s + 2)
                    elif kind == "ln1_stats" and attend:
                        if n == 0:
                            dve.wait_ge(residual, KT * (a + 1))
                        ln_stats(1, x_res[:, par, :, :], n, a + 1)
                    elif kind == "ln1_scale" and attend:
                        ln_scales(1, a + 1)

            turns(dve, turn)

        @block.tensor
        def _(pe):
            def product(dst, left, right, pairs):
                for n, (i, j) in enumerate(pairs):
                    ins = nc.tensor.matmul(dst, left(i), right(j), start=(n == 0), stop=(n == len(pairs) - 1))
                return ins

            over_features = [((h1_, k), (h2_, k)) for k in range(KT) for h1_, h2_ in SPLIT]

            def col(n, size=P):
                return slice(n * size, (n + 1) * size)

            def h_transposed(n, dst):
                for t in range(TILES):
                    ins = nc.tensor.transpose(dst[:, col(t)], h[:, t, col(n)], ident[:, :])
                return ins

            pe.wait_ge(consts_ready, 2)
            pe.wait_ge(ln_done[0], TILES)
            for n in range(KT):
                need(pe, p_done, n - 1)
                h_transposed(n, PB[n % 2]).then_inc(p_product, 1)

            def setup_chunk(step):
                kind, n = step
                c = SETUP.index(step)
                dst = RB[c % 2]
                need(pe, setup_done, c - 1)
                if kind == "rq":
                    if n == 0:
                        pe.wait_ge(w_loaded[4], 16)
                        pe.wait_ge(w_loaded[5], 16)
                    for k in range(KT):
                        ins = nc.tensor.matmul(dst[:, :], stage[1][:, k, col(n)], stage[2][:, k, :],
                                               start=(k == 0), stop=(k == KT - 1))
                elif kind == "rv":
                    if n == 0:
                        pe.wait_ge(w_loaded[3], 16)
                    for k in range(KT):
                        ins = nc.tensor.transpose(dst[:, col(k)], stage[0][:, k, col(n)], ident[:, :])
                else:
                    pe.wait_ge(adj_loaded, 16)
                    for i in range(NT):
                        for j in range(NT):
                            ins = nc.tensor.transpose(dst[:, i * N + j * P:i * N + (j + 1) * P],
                                                      adj_in[:, j, col(i)], ident[:, :])
                ins.then_inc(setup_product, 1)

            def turn(s, odd):
                project, attend, relate, ln0, _ = stages(s, PAIRS)
                a, l = s - 1, s - 2
                par = 1 - odd
                for kind, n in PLAN:
                    if (kind in ("q", "k", "v") and project) or (kind == "ht" and ln0):
                        c = in_project((kind, n), ln0)
                        dst = PB[c % 2]
                        need(pe, p_done, before_project(s) + c - 1)
                        if kind == "ht":
                            if n == 0:
                                pe.wait_ge(ln_done[0], TILES * (s + 2))
                            ins = h_transposed(n, dst)
                        elif kind == "v":
                            if n == 0:
                                first = isinstance(s, int) and s == 0
                                if first:
                                    pe.wait_ge(w_low, 1)
                                pe.wait_ge(p_done, KT if first else
                                           before_project(s - 1) + PROJECT.index(("ht", KT - 1)) + 1)
                            ins = product(dst[:, :], lambda i: h0t[:, odd, i[0], i[1], col(n)],
                                          lambda j: wv[:, j[0], j[1], :], over_features)
                        else:
                            if isinstance(s, int) and s == 0 and n == 0:
                                pe.wait_ge(w_low, 2 if kind == "q" else 3)
                            w = wq if kind == "q" else wk
                            ins = product(dst[:, :], lambda i: w[:, i[0], i[1], col(n)],
                                          lambda j: h0t[:, odd, j[0], j[1], :], over_features)
                        ins.then_inc(p_product, 1)
                    elif kind == "scores" and attend:
                        m, g, e = unit(n)
                        if n % 4 == 0:
                            pe.wait_ge(k_doubled[m], 32 * (a + 1))
                        need(pe, maxed, UNITS * a + n - 1)
                        for i in range(NT):
                            ins = product(S[n % 2][:, i, :], lambda _: q_st[:, m, e, col(g * NT + i)],
                                          lambda h: k_st[:, m, e, h, col(g, N)], [(0, 0), (0, 1)])
                        ins.then_inc(scored, 1)
                    elif kind == "probs_t" and attend:
                        pe.wait_ge(exped, UNITS * a + n + 1)
                        need(pe, pt_low, UNITS * a + n)
                        for i in range(NT):
                            for j in range(NT):
                                ins = nc.tensor.transpose(PT[:, j, col(i)], probs[:, n % 4, i, col(j)], ident[:, :])
                        ins.then_inc(transposed, 1)
                    elif kind == "pv" and attend:
                        m, g, e = unit(n)
                        if n == 0:
                            pe.wait_ge(v_low, TILES * (a + 1))
                        if n % 4 == 0:
                            need(pe, normed, KT * a + m)
                        pe.wait_ge(pt_low, UNITS * a + n + 1)
                        for i in range(NT):
                            ins = product(O[:, (g * NT + i) * 2 + e, :],
                                          lambda k: probs_t[:, n % 2, k[0], k[1], col(i)],
                                          lambda k: v[:, par, k[0], g * NT + k[1], col(2 * m + e, HD)],
                                          [((h1_, j), (h2_, j)) for j in range(NT) for h1_, h2_ in SPLIT])
                        ins.then_inc(summed, 1)
                    elif (kind, n) in SETUP and isinstance(s, int) and s == 1:
                        setup_chunk((kind, n))
                    elif kind in ("rht", "rq", "rv", "rel", "relt", "out") and relate:
                        c = RELATE.index((kind, n))
                        dst = RB[c % 2]
                        if isinstance(s, int) and s == 2 and c == 0:
                            pe.wait_ge(setup_done, NSETUP)
                        need(pe, r_done, NRC * l + c - 1)
                        if kind == "rht":
                            if n == 0:
                                pe.wait_ge(ln_done[1], TILES * (l + 1))
                            ins = h_transposed(n, dst)
                        elif kind == "rq":
                            if n == 0:
                                pe.wait_ge(r_done, NRC * l + RELATE.index(("rht", KT - 1)) + 1)
                            ins = product(dst[:, :], lambda i: wm[:, i[0], i[1], col(n)],
                                          lambda j: h1t[:, j[0], j[1], :], over_features)
                        elif kind == "rv":
                            ins = product(dst[:, :], lambda i: h1t[:, i[0], i[1], col(n)],
                                          lambda j: wvt[:, j[0], j[1], :], over_features)
                        elif kind == "rel":
                            if n == 0:
                                pe.wait_ge(r_done, NRC * l + RELATE.index(("rq", KT - 1)) + 1)
                            for i in range(NT):
                                ins = product(dst[:, col(i, N)], lambda k: rq[:, k[0], k[1], col(n * NT + i)],
                                              lambda k: h1t[:, k[0], k[1], col(n, N)], over_features)
                        elif kind == "relt":
                            pe.wait_ge(rel_normed, 2 * l + n + 1)
                            for j in range(NT):
                                for i in range(NT):
                                    ins = nc.tensor.transpose(dst[:, j * N + i * P:j * N + (i + 1) * P],
                                                              rel_n[:, n, i, col(j)], ident[:, :])
                        else:
                            g, i = n // NT, n % NT
                            if i == 0:
                                pe.wait_ge(r_done, NRC * l + 1 + max(RELATE.index(("relt", g)),
                                                                     RELATE.index(("rv", g * NT + NT - 1))))
                            ins = product(dst[:, :], lambda k: rel_t[:, g, k[0], k[1], col(i)],
                                          lambda k: rv[:, k[0], g * NT + k[1], :],
                                          [((h1_, j), (h2_, j)) for j in range(NT) for h1_, h2_ in SPLIT])
                        ins.then_inc(r_product, 1)

            turns(pe, turn)


_INS = ['x', 'adj', 'L0_gnn_Wq', 'L0_gnn_bq', 'L0_gnn_Wk', 'L0_gnn_bk', 'L0_gnn_Wv', 'L0_gnn_bv',
        'L1_gnn_Wq', 'L1_gnn_Wk', 'L1_gnn_Wv']


def kernel(**inputs):
    import numpy as _np
    import concourse.bacc as _bacc
    from concourse import mybir as _mybir
    from concourse.bass_utils import run_bass_kernel_spmd as _run

    nc = _bacc.Bacc("TRN2", target_bir_lowering=False, num_devices=1)
    arrays, args = {}, []
    for name in _INS:
        a = _np.ascontiguousarray(inputs[name])
        arrays[f"in_{name}_dram"] = a
        args.append(nc.dram_tensor(f"in_{name}_dram", a.shape, _mybir.dt.from_np(a.dtype), kind="ExternalInput").ap())
    shape = inputs['x'].shape
    args.append(nc.dram_tensor("out_0_dram", shape, _mybir.dt.float32, kind="ExternalOutput").ap())
    adjacency_attention_two_layers(nc, *args)
    r = _run(nc, [arrays], core_ids=[0])
    return r.results[0]["out_0_dram"]
```
